# Optimizing a Trainium2 kernel written in Bass

```python
import numpy as np
import jax
import jax.numpy as jnp

def _softmax(x, axis=-1):
    return jax.nn.softmax(x, axis=axis)

def _gelu(x):
    return jax.nn.gelu(x, approximate=True)

def _silu(x):
    return jax.nn.silu(x)

def _sigmoid(x):
    return jax.nn.sigmoid(x)

def _layernorm(x, axis=-1, eps=1e-05):
    m = jnp.mean(x, axis=axis, keepdims=True)
    v = jnp.var(x, axis=axis, keepdims=True)
    return (x - m) / jnp.sqrt(v + eps)

def _scatter_add(tgt, idx, src, axis=0):
    return tgt.at[idx].add(src)

def _segment_sum(src, seg, n):
    return jax.ops.segment_sum(src, seg, n)
kernel_name = 'mk_vit_tower_d1_tok_img256_r4_95c74d'

def setup_inputs(seed: int=0):
    np.random.seed(seed)
    _w = jnp.asarray

    def _rec_inputs():
        import jax
        import jax.numpy as jnp
        _rk = jax.random.key(seed)
        x = 7.22013e-05 + 1.00017 * jax.random.normal(jax.random.fold_in(_rk, 1), (16, 1, 1024, 64), jnp.float32)
        return x
    x = _rec_inputs()

    def _L0_tok_setup():
        import jax, jax.numpy as jnp
        import numpy as np
        T, D_IN, D_INT, D_OUT, B = (1024, 64, 64, 64, 8)
        key = jax.random.key(seed)
        ks = jax.random.split(key, 12)
        s_in = 1.0 / np.sqrt(D_IN)
        s_int = 1.0 / np.sqrt(D_INT)
        return {'x_batched': jax.random.normal(ks[0], (B, 1, T, D_IN), dtype=jnp.float32), 'd_gamma_batched': jax.random.uniform(ks[1], (T, T), dtype=jnp.float32), 'Wq': jax.random.uniform(ks[2], (D_IN, D_INT), jnp.float32, -s_in, s_in), 'bq': jax.random.uniform(ks[3], (D_INT,), jnp.float32, -s_in, s_in), 'Wk': jax.random.uniform(ks[4], (D_IN, D_INT), jnp.float32, -s_in, s_in), 'bk': jax.random.uniform(ks[5], (D_INT,), jnp.float32, -s_in, s_in), 'Wv': jax.random.uniform(ks[6], (D_IN, D_INT), jnp.float32, -s_in, s_in), 'bv': jax.random.uniform(ks[7], (D_INT,), jnp.float32, -s_in, s_in), 'Wo': jax.random.uniform(ks[8], (D_INT, D_OUT), jnp.float32, -s_int, s_int), 'bo': jax.random.uniform(ks[9], (D_OUT,), jnp.float32, -s_int, s_int), 'prelu_a': jnp.float32(0.25)}
    _L0_tok_all = _L0_tok_setup()
    _L0_tok_in = {k: v for k, v in _L0_tok_all.items() if k in ('d_gamma_batched', 'Wq', 'bq', 'Wk', 'bk', 'Wv', 'bv', 'Wo', 'bo', 'prelu_a')}
    del _L0_tok_all

    def _L0_attn_setup():
        import jax, jax.numpy as jnp
        import numpy as np
        B, T, F, H = (128, 256, 64, 128)

        def _lstm(xWb, U, reverse=False, return_sequences=False):
            Hn = U.shape[0]
            xs = jnp.swapaxes(xWb, 0, 1)
            h0 = jnp.zeros((xWb.shape[0], Hn), xWb.dtype)
            c0 = h0

            def step(carry, xw):
                h, c = carry
                z = xw + h @ U
                i, f, g, o = jnp.split(z, 4, axis=-1)
                i = jax.nn.sigmoid(i)
                f = jax.nn.sigmoid(f)
                g = jnp.tanh(g)
                o = jax.nn.sigmoid(o)
                c = f * c + i * g
                h = o * jnp.tanh(c)
                return ((h, c), h)
            (hT, _), hs = jax.lax.scan(step, (h0, c0), xs, reverse=reverse)
            if return_sequences:
                return jnp.swapaxes(hs, 0, 1)
            return hT
        key = jax.random.key(seed)
        ks = jax.random.split(key, 9)
        g = lambda k, shape: jax.random.normal(k, shape, jnp.float32) * 0.05
        return {'x': jax.random.uniform(ks[0], (B, T, F), jnp.float32), 'Wf': g(ks[1], (F, 4 * H)), 'Uf': g(ks[2], (H, 4 * H)), 'bf': jnp.zeros((4 * H,), jnp.float32), 'Wb': g(ks[3], (F, 4 * H)), 'Ub': g(ks[4], (H, 4 * H)), 'bb': jnp.zeros((4 * H,), jnp.float32), 'Wd': g(ks[5], (2 * H, 4 * H)), 'Ud': g(ks[6], (H, 4 * H)), 'bd': jnp.zeros((4 * H,), jnp.float32), 'Wo': g(ks[7], (H, F)), 'bo': jnp.zeros((F,), jnp.float32)}
    _L0_attn_all = _L0_attn_setup()
    _L0_attn_in = {k: v for k, v in _L0_attn_all.items() if k in ('Wf', 'Uf', 'bf', 'Wb', 'Ub', 'bb', 'Wd', 'Ud', 'bd', 'Wo', 'bo')}
    del _L0_attn_all

    def _L0_ffn_setup():
        import jax, jax.numpy as jnp
        import numpy as np
        B, S, D, E, H, K = (4, 1024, 64, 8, 128, 2)
        key = jax.random.key(seed)
        ks = jax.random.split(key, 6)
        x = jax.random.normal(ks[0], (B, S, D), jnp.float32)
        Wg = jax.random.normal(ks[1], (D, E), jnp.float32) * 0.02
        bg = jnp.zeros((E,), jnp.float32)
        W1 = jax.random.normal(ks[2], (E, D, H), jnp.float32) * 0.02
        b1 = jnp.zeros((E, H), jnp.float32)
        W2 = jax.random.normal(ks[3], (E, H, D), jnp.float32) * 0.02
        b2 = jnp.zeros((E, D), jnp.float32)
        return {'x': x, 'Wg': Wg, 'bg': bg, 'W1': W1, 'b1': b1, 'W2': W2, 'b2': b2}
    _L0_ffn_all = _L0_ffn_setup()
    _L0_ffn_in = {k: v for k, v in _L0_ffn_all.items() if k in ('Wg', 'bg', 'W1', 'b1', 'W2', 'b2')}
    del _L0_ffn_all
    return {'x': x, 'L0_tok_d_gamma_batched': _L0_tok_in['d_gamma_batched'], 'L0_tok_Wq': _L0_tok_in['Wq'], 'L0_tok_bq': _L0_tok_in['bq'], 'L0_tok_Wk': _L0_tok_in['Wk'], 'L0_tok_bk': _L0_tok_in['bk'], 'L0_tok_Wv': _L0_tok_in['Wv'], 'L0_tok_bv': _L0_tok_in['bv'], 'L0_tok_Wo': _L0_tok_in['Wo'], 'L0_tok_bo': _L0_tok_in['bo'], 'L0_tok_prelu_a': _L0_tok_in['prelu_a'], 'L0_attn_Wf': _L0_attn_in['Wf'], 'L0_attn_Uf': _L0_attn_in['Uf'], 'L0_attn_bf': _L0_attn_in['bf'], 'L0_attn_Wb': _L0_attn_in['Wb'], 'L0_attn_Ub': _L0_attn_in['Ub'], 'L0_attn_bb': _L0_attn_in['bb'], 'L0_attn_Wd': _L0_attn_in['Wd'], 'L0_attn_Ud': _L0_attn_in['Ud'], 'L0_attn_bd': _L0_attn_in['bd'], 'L0_attn_Wo': _L0_attn_in['Wo'], 'L0_attn_bo': _L0_attn_in['bo'], 'L0_ffn_Wg': _L0_ffn_in['Wg'], 'L0_ffn_bg': _L0_ffn_in['bg'], 'L0_ffn_W1': _L0_ffn_in['W1'], 'L0_ffn_b1': _L0_ffn_in['b1'], 'L0_ffn_W2': _L0_ffn_in['W2'], 'L0_ffn_b2': _L0_ffn_in['b2']}

def reference(x, L0_tok_d_gamma_batched, L0_tok_Wq, L0_tok_bq, L0_tok_Wk, L0_tok_bk, L0_tok_Wv, L0_tok_bv, L0_tok_Wo, L0_tok_bo, L0_tok_prelu_a, L0_attn_Wf, L0_attn_Uf, L0_attn_bf, L0_attn_Wb, L0_attn_Ub, L0_attn_bb, L0_attn_Wd, L0_attn_Ud, L0_attn_bd, L0_attn_Wo, L0_attn_bo, L0_ffn_Wg, L0_ffn_bg, L0_ffn_W1, L0_ffn_b1, L0_ffn_W2, L0_ffn_b2):
    import jax
    import jax.numpy as jnp

    def _L0_tok_ref(x_batched, d_gamma_batched, Wq, bq, Wk, bk, Wv, bv, Wo, bo, prelu_a):
        import jax, jax.numpy as jnp
        import numpy as np
        T, D_IN, D_INT, D_OUT, B = (1024, 64, 64, 64, 8)
        x = x_batched.reshape(x_batched.shape[0], T, D_IN)
        q = x @ Wq + bq
        k = x @ Wk + bk
        v = x @ Wv + bv
        scores = jnp.einsum('btd,bsd->bts', q, k)
        retained = jnp.einsum('bts,bsd->btd', d_gamma_batched * scores, v)
        y = retained @ Wo + bo
        out = jnp.where(y >= 0, y, prelu_a * y)
        return out

    def _L0_attn_ref(x, Wf, Uf, bf, Wb, Ub, bb, Wd, Ud, bd, Wo, bo):
        import jax, jax.numpy as jnp
        import numpy as np
        B, T, F, H = (128, 256, 64, 128)

        def _lstm(xWb, U, reverse=False, return_sequences=False):
            Hn = U.shape[0]
            xs = jnp.swapaxes(xWb, 0, 1)
            h0 = jnp.zeros((xWb.shape[0], Hn), xWb.dtype)
            c0 = h0

            def step(carry, xw):
                h, c = carry
                z = xw + h @ U
                i, f, g, o = jnp.split(z, 4, axis=-1)
                i = jax.nn.sigmoid(i)
                f = jax.nn.sigmoid(f)
                g = jnp.tanh(g)
                o = jax.nn.sigmoid(o)
                c = f * c + i * g
                h = o * jnp.tanh(c)
                return ((h, c), h)
            (hT, _), hs = jax.lax.scan(step, (h0, c0), xs, reverse=reverse)
            if return_sequences:
                return jnp.swapaxes(hs, 0, 1)
            return hT
        h_fwd = _lstm(x @ Wf + bf, Uf, reverse=False)
        h_bwd = _lstm(x @ Wb + bb, Ub, reverse=True)
        latent = jnp.concatenate([h_fwd, h_bwd], axis=-1)
        rep = jnp.broadcast_to(latent[:, None, :], (x.shape[0], x.shape[1], 2 * H))
        dec = _lstm(rep @ Wd + bd, Ud, return_sequences=True)
        return dec @ Wo + bo

    def _L0_ffn_ref(x, Wg, bg, W1, b1, W2, b2):
        import jax, jax.numpy as jnp
        import numpy as np
        B, S, D, E, H, K = (4, 1024, 64, 8, 128, 2)
        Bv, Sv, Dv = x.shape
        gate_scores = x @ Wg + bg
        _, idx = jax.lax.top_k(gate_scores, K)
        mask = jax.nn.one_hot(idx, E, dtype=x.dtype).sum(axis=-2)
        xf = x.reshape(-1, Dv)
        mf = mask.reshape(-1, E)
        h = jax.nn.gelu(jnp.einsum('td,edh->teh', xf, W1) + b1[None], approximate=False)
        y = jnp.einsum('teh,ehd->ted', h, W2) + b2[None]
        out = jnp.einsum('ted,te->td', y, mf)
        return out.reshape(Bv, Sv, Dv)
    h = _L0_tok_ref(x, L0_tok_d_gamma_batched, L0_tok_Wq, L0_tok_bq, L0_tok_Wk, L0_tok_bk, L0_tok_Wv, L0_tok_bv, L0_tok_Wo, L0_tok_bo, L0_tok_prelu_a)
    h = h + _L0_attn_ref(_layernorm(h, axis=-1), L0_attn_Wf, L0_attn_Uf, L0_attn_bf, L0_attn_Wb, L0_attn_Ub, L0_attn_bb, L0_attn_Wd, L0_attn_Ud, L0_attn_bd, L0_attn_Wo, L0_attn_bo)
    h = h + _L0_ffn_ref(_layernorm(h, axis=-1), L0_ffn_Wg, L0_ffn_bg, L0_ffn_W1, L0_ffn_b1, L0_ffn_W2, L0_ffn_b2)
    return h

_drawn_inputs = setup_inputs


def setup_inputs(seed=0):
    import zlib

    import numpy as np

    out = dict(_drawn_inputs(seed))
    spreads = {'L0_attn_bf': (0.0, 0.8),
     'L0_attn_bb': (0.0, 0.8),
     'L0_attn_bd': (0.0, 0.8),
     'L0_attn_bo': (0.0, 2.0),
     'L0_ffn_bg': (0.0, 0.8),
     'L0_ffn_b1': (0.0, 2.0),
     'L0_ffn_b2': (0.0, 2.0)}
    factors = {'L0_tok_bo': 8.0,
     'L0_attn_Wf': 8.0,
     'L0_attn_Uf': 8.0,
     'L0_attn_Wb': 8.0,
     'L0_attn_Ub': 8.0,
     'L0_attn_Wd': 8.0,
     'L0_attn_Ud': 8.0,
     'L0_attn_Wo': 8.0,
     'L0_ffn_Wg': 8.0,
     'L0_ffn_W1': 8.0,
     'L0_ffn_W2': 8.0}
    for name, (base, spread) in spreads.items():
        noise = np.random.default_rng([zlib.crc32(name.encode()), seed]).standard_normal(out[name].shape)
        drawn = base * np.exp(spread * noise) if base else spread * noise
        out[name] = jnp.asarray(drawn.astype(out[name].dtype))
    for name, factor in factors.items():
        out[name] = (out[name] * factor).astype(out[name].dtype)
    return out
```

```python
from contextlib import ExitStack

import numpy as np
import concourse.bass as bass
from concourse import mybir

F32, F16, BF16 = mybir.dt.float32, mybir.dt.float16, mybir.dt.bfloat16
ALU = mybir.AluOpType
ACT = mybir.ActivationFunctionType
AX = mybir.AxisListType

P = 128
B, T, D = 16, 1024, 64
H = 128
E, HE = 8, 128
NB = T // P
HALF = 512
EPS = 1e-5

W_SCALE = 2.0 ** 6
X_SCALE = 2.0 ** 12
Z_SCALE = W_SCALE * X_SCALE
F_, G_, I_, O_ = range(4)
GATE_FROM = (1, 2, 0, 3)
GATE_SCALE = (0.5 * W_SCALE, W_SCALE, 0.5 * W_SCALE, 0.5 * W_SCALE)

CH = 16
COLS = CH * B
NCH = T // CH
HALFCH = COLS // 2
BIG = 2.0 ** 100


def tools(nc):
    ctx = ExitStack()
    return (ctx, lambda name, shape, dt: ctx.enter_context(nc.sbuf_tensor(name, shape, dt)),
            lambda name: ctx.enter_context(nc.semaphore(name)))


class Links:

    def __init__(self, engine, sem, base=0):
        self.engine, self.sem, self.base, self.n = engine, sem, base, 0

    def link(self, instruction):
        instruction.then_inc(self.sem, 1)
        self.n += 1
        self.engine.wait_ge(self.sem, self.base + self.n)


class Shared:
    pass


def build(nc, a, out):
    ctx = ExitStack()
    m = Shared()
    m.a, m.out = a, out

    def sb(name, shape, dt):
        return ctx.enter_context(nc.sbuf_tensor(name, shape, dt))

    with ctx:
        m.bank = [ctx.enter_context(nc.psum_tensor(f"bank{k}", [P, HALF], F32)) for k in range(8)]
        m.ident = sb("ident", [P, P], F32)
        m.ident16 = sb("ident16", [P, P], F16)
        m.identb = sb("identb", [P, P], BF16)
        m.res = sb("res", [P, B, NB, D], F32)
        m.gamma_or_h = sb("gamma_or_h", [P, NB * T], F32)
        m.gT = m.gamma_or_h[:, :].rearrange("p (s t) -> p s t", s=NB)
        m.dec_hi = m.gamma_or_h[:, :].bitcast(F16)
        m.xs = sb("xs", [P, T * B + 2 * COLS], F16)
        m.dec_lo = m.xs[:, COLS:COLS + T * B]
        m.u_hi = [sb(f"u_hi{d}", [P, 4, H], F16) for d in range(3)]
        m.u_lo = [sb(f"u_lo{d}", [P, 4, H], F16) for d in range(3)]
        m.w_hi = [sb(f"w_hi{d}", [P, 4, H], F16) for d in range(2)]
        m.w_lo = [sb(f"w_lo{d}", [P, 4, H], F16) for d in range(2)]
        m.wd_hi = [sb(f"wd_hi{d}", [P, 4, H], F16) for d in range(2)]
        m.wd_lo = [sb(f"wd_lo{d}", [P, 4, H], F16) for d in range(2)]
        m.bias = sb("bias", [3, 3 * 4 * H + D + E], BF16)
        m.lstm_bias = [m.bias[:, 4 * H * d:4 * H * (d + 1)].rearrange("p (g h) -> p g h", g=4)
                       for d in range(3)]
        m.wo_bias = m.bias[:, 12 * H:12 * H + D]
        m.gate_bias = m.bias[:, 12 * H + D:12 * H + D + E]
        m.ones3 = sb("ones3", [3, P], BF16)
        m.a_col = sb("a_col", [P, 1], F32)
        m.bo_col = sb("bo_col", [P, 1], F32)
        m.wo_hi = sb("wo_hi", [P, D], F16)
        m.wo_lo = sb("wo_lo", [P, D], F16)
        m.wg_hi = sb("wg_hi", [P, E], F16)
        m.wg_lo = sb("wg_lo", [P, E], F16)
        m.w1_hi = sb("w1_hi", [P, E, HE], F16)
        m.w1_lo = sb("w1_lo", [P, E, HE], F16)
        m.w2 = sb("w2", [HE, E, D], F32)
        m.b1 = sb("b1", [HE, E], F32)
        m.b2 = sb("b2", [2 * E, 3, D], BF16)
        m.pick = sb("pick", [2 * E, E, HE], BF16)
        m.wq = sb("wq", [D + 1, D], F32)
        m.wk = sb("wk", [D + 1, D], F32)
        m.wvo = sb("wvo", [D + 1, D], F32)
        m.enc_hi = [sb(f"enc_hi{d}", [P, B], F16) for d in range(2)]
        m.enc_lo = [sb(f"enc_lo{d}", [P, B], F16) for d in range(2)]

        for phase in (setup, token_mixing, encoder, decoder):
            phase(nc, m)
        m.xn = sb("xn", [P, B * T], F16)
        m.mask = sb("mask", [P, B, NB, 2 * E], BF16)
        for phase in (project_and_route, experts):
            phase(nc, m)


def setup(nc, m):
    a = m.a
    ctx, sb, sem = tools(nc)
    NBIAS = 12 * H + D + E
    with ctx:
        raw_u = [sb(f"raw_u{d}", [P, 4 * H], F32) for d in range(3)]
        raw_w = [sb(f"raw_w{d}", [P, 4 * H], F32) for d in range(2)]
        raw_wd = [sb(f"raw_wd{d}", [P, 4 * H], F32) for d in range(2)]
        raw_wo = sb("raw_wo", [P, D], F32)
        raw_wg = sb("raw_wg", [P, E], F32)
        raw_first = sb("raw_first", [P, E, HE], F32)
        raw_b = sb("raw_b", [3, NBIAS], F32)
        part = sb("part", [3, 3, NBIAS], BF16)
        left = sb("left", [3, 3, NBIAS], F32)
        raw_b2 = sb("raw_b2", [2 * E, 3, D], F32)
        wv = sb("wv", [D + 1, D], F32)
        tok_wo = sb("tok_wo", [D, D], F32)
        wvT = sb("wvT", [D, D + 1], F32)
        g_rows = [sb(f"g_rows{k}", [P, T], F32) for k in range(2)]
        s_w, s_b, s_dve, s_z, s_id, s_id0 = (sem(n) for n in
            ("weights_loaded", "vectors_loaded", "split_step", "b2_zeroed", "ident_made", "ident_zeroed"))
        s_g = [sem(f"gamma_loaded{k}") for k in range(2)]
        s_gt, s_gfree, s_v, s_vk = (sem(n) for n in
            ("gamma_turned", "gamma_banks_free", "wv_on_pe", "wv_kept"))
        n_w, n_b = [0], [0]


        with nc.Block() as block:
            @block.sync
            def _(sp):
                def load(dst, src, s=s_w, n=n_w, scattered=False):
                    sp.dma_start(dst, src, allow_slow_non_contiguous=scattered).then_inc(s, 16)
                    n[0] += 16

                for k in range(2):
                    sp.dma_start(g_rows[k][:], a["L0_tok_d_gamma_batched"][k * P:(k + 1) * P, :]).then_inc(s_g[k], 16)
                load(wv[0:D, :], a["L0_tok_Wv"])
                load(wv[D:D + 1, :], a["L0_tok_bv"][None, :])
                load(tok_wo[:], a["L0_tok_Wo"])
                load(m.wq[0:D, :], a["L0_tok_Wq"])
                load(m.wq[D:D + 1, :], a["L0_tok_bq"][None, :])
                load(m.wk[0:D, :], a["L0_tok_Wk"])
                load(m.wk[D:D + 1, :], a["L0_tok_bk"][None, :])
                for k in range(2):
                    load(m.bo_col[k * D:(k + 1) * D, :], a["L0_tok_bo"][:, None])
                load(m.a_col[:], a["L0_tok_prelu_a"][None, :].broadcast_to([P, 1]))
                for d, u in enumerate((a["L0_attn_Uf"], a["L0_attn_Ub"], a["L0_attn_Ud"])):
                    load(raw_u[d][:], u)
                for d, w in enumerate((a["L0_attn_Wf"], a["L0_attn_Wb"])):
                    load(raw_w[d][0:D, :], w)
                    load(raw_w[d][D:2 * D, :], w)
                for d in range(2):
                    load(raw_wd[d][:], a["L0_attn_Wd"][H * d:H * (d + 1), :])
                load(raw_wo[:], a["L0_attn_Wo"])
                for k in range(2):
                    load(raw_wg[k * D:(k + 1) * D, :], a["L0_ffn_Wg"])
                    load(raw_first[k * D:(k + 1) * D, :, :], a["L0_ffn_W1"].rearrange("e d h -> d e h"))
                load(m.w2[:], a["L0_ffn_W2"].rearrange("e h d -> h e d"))
                load(m.b1[:], a["L0_ffn_b1"].rearrange("e h -> h e"), scattered=True)
                for row in range(3):
                    for d, b in enumerate((a["L0_attn_bf"], a["L0_attn_bb"], a["L0_attn_bd"])):
                        for g in range(4):
                            k = (4 * d + g) * H
                            load(raw_b[row:row + 1, k:k + H],
                                 b[None, GATE_FROM[g] * H:(GATE_FROM[g] + 1) * H], s_b, n_b)
                    load(raw_b[row:row + 1, 12 * H:12 * H + D], a["L0_attn_bo"][None, :], s_b, n_b)
                    load(raw_b[row:row + 1, 12 * H + D:], a["L0_ffn_bg"][None, :], s_b, n_b)
                sp.wait_ge(s_z, 1)
                load(raw_b2[E:2 * E, 0, :], a["L0_ffn_b2"], s_b, n_b)
                with sp.Fori(0, NB // 2 - 1) as i:
                    for k in range(2):
                        sp.wait_ge(s_gt, 4 * i + 2 * k + 2)
                        sp.dma_start(g_rows[k][:], a["L0_tok_d_gamma_batched"][bass.ds((2 * i + k + 2) * P, P), :]
                                     ).then_inc(s_g[k], 16)

            @block.gpsimd
            def _(pool):
                nc.gpsimd.memset(m.ident[:], 0.0).then_inc(s_id0, 1)
                pool.wait_ge(s_id0, 1)
                nc.gpsimd.affine_select(out=m.ident[:], in_=m.ident[:], compare_op=ALU.not_equal, fill=1.0,
                                        base=0, pattern=[[-1, P]], channel_multiplier=1).then_inc(s_id, 1)
                nc.gpsimd.memset(raw_b2[:], 0.0).then_inc(s_z, 1)
                nc.gpsimd.memset(m.ones3[:], Z_SCALE)
                nc.gpsimd.memset(m.xs[:, 0:COLS], 0.0)
                nc.gpsimd.memset(m.xs[:, COLS + T * B:], 0.0)

            @block.tensor
            def _(pe):
                pe.wait_ge(s_id, 1)
                with pe.Fori(0, NB // 2) as i:
                    for k in range(2):
                        pe.wait_ge(s_g[k], 16 * i + 16)
                        for half in range(2):
                            pe.wait_ge(s_gfree, 4 * i + 2 * k + half + 1)
                            for s in range(4):
                                blk = 4 * half + s
                                last = nc.tensor.transpose(m.bank[2 * k + half][:, s * P:(s + 1) * P],
                                                           g_rows[k][:, blk * P:(blk + 1) * P], m.ident[:])
                            last.then_inc(s_gt, 1)
                pe.wait_ge(s_w, n_w[0])
                nc.tensor.transpose(m.bank[4][0:D, 0:D + 1], wv[:], m.ident[0:D + 1, 0:D + 1]).then_inc(s_v, 1)
                pe.wait_ge(s_vk, 1)
                nc.tensor.matmul(m.bank[5][0:D + 1, 0:D], wvT[:], tok_wo[:], start=True, stop=True).then_inc(s_v, 1)

            @block.scalar
            def _(act):
                act.wait_ge(s_id, 1)
                nc.scalar.copy(wvT[:], m.ident[0:D, 0:D + 1]).then_inc(s_gfree, 4)
                with act.Fori(0, NB // 2) as i:
                    for k in range(2):
                        for half in range(2):
                            act.wait_ge(s_gt, 4 * i + 2 * k + half + 1)
                            nc.scalar.copy(m.gT[:, 4 * half:4 * half + 4, bass.ds((2 * i + k) * P, P)],
                                           m.bank[2 * k + half][:].rearrange("p (s t) -> p s t", s=4)
                                           ).then_inc(s_gfree, 1)
                act.wait_ge(s_v, 1)
                nc.scalar.copy(wvT[:], m.bank[4][0:D, 0:D + 1]).then_inc(s_vk, 1)
                act.wait_ge(s_v, 2)
                nc.scalar.copy(m.wvo[:], m.bank[5][0:D + 1, 0:D])

            @block.vector
            def _(dve):
                own = Links(dve, s_dve)
                V = nc.vector
                dve.wait_ge(s_id, 1)
                V.tensor_copy(m.ident16[:], m.ident[:])
                V.tensor_copy(m.identb[:], m.ident[:])
                V.tensor_scalar(m.pick[:], m.ident[0:2 * E, 0:E].unsqueeze(2).broadcast_to([2 * E, E, HE]), BIG, None, ALU.mult)
                dve.wait_ge(s_w, n_w[0])

                def split(high, low, raw, scale):
                    own.link(V.tensor_scalar(high, raw, scale, None, ALU.mult))
                    V.scalar_tensor_tensor(low, raw, scale, high, ALU.mult, ALU.subtract)

                lstm = ([(m.u_hi[d], m.u_lo[d], raw_u[d]) for d in range(3)]
                        + [(m.w_hi[d], m.w_lo[d], raw_w[d]) for d in range(2)]
                        + [(m.wd_hi[d], m.wd_lo[d], raw_wd[d]) for d in range(2)])
                for high, low, raw in lstm:
                    for g in range(4):
                        k = GATE_FROM[g] * H
                        split(high[:, g, :], low[:, g, :], raw[:, k:k + H], GATE_SCALE[g])
                split(m.wo_hi[:], m.wo_lo[:], raw_wo[:], W_SCALE)
                split(m.wg_hi[:], m.wg_lo[:], raw_wg[:], W_SCALE)
                split(m.w1_hi[:], m.w1_lo[:], raw_first[:], W_SCALE)

                dve.wait_ge(s_b, n_b[0])
                for d in range(3):
                    for g in (F_, I_, O_):
                        k = (4 * d + g) * H
                        last = V.tensor_scalar(raw_b[:, k:k + H], raw_b[:, k:k + H], 0.5, None, ALU.mult)
                own.link(last)

                def thirds(value, part, left):
                    own.link(V.tensor_copy(part[:, 0], value))
                    own.link(V.tensor_tensor(left[:, 0], value, part[:, 0], ALU.subtract))
                    own.link(V.tensor_copy(part[:, 1], left[:, 0]))
                    own.link(V.tensor_tensor(left[:, 1], left[:, 0], part[:, 1], ALU.subtract))
                    own.link(V.tensor_copy(part[:, 2], left[:, 1]))

                thirds(raw_b[:], part, left)
                own.link(V.tensor_scalar(left[:, 0], part[:, 0], m.ident[0:3, 0:1], None, ALU.mult))
                own.link(V.scalar_tensor_tensor(left[:, 1], part[:, 1], m.ident[0:3, 1:2], left[:, 0],
                                                ALU.mult, ALU.add))
                V.scalar_tensor_tensor(m.bias[:], part[:, 2], m.ident[0:3, 2:3], left[:, 1], ALU.mult, ALU.add)
                thirds(raw_b2[:, 0, :], m.b2, raw_b2[:, 1:3, :])


TOKENS_OF = [4 * (q % 2) + q // 2 for q in range(NB)]
MASK_OF = [TOKENS_OF.index(c) for c in range(NB)]
LN_LINKS = 12


class Layernorm:

    def __init__(self, sb, name):
        one = lambda part: sb(name + part, [P, NB], F32)
        self.h, self.centred, self.square = (sb(name + part, [P, NB, D], F32) for part in ("h", "centred", "square"))
        self.split = sb(name + "split", [P, NB, 2 * D], F16)
        self.total, self.mean, self.squares, self.var, self.dev = (one(p) for p in
                                                                   ("total", "mean", "squares", "var", "dev"))
        self.r0, self.t1, self.t2, self.t3, self.r = (one(p) for p in ("r0", "t1", "t2", "t3", "r"))


def over_tokens(column):
    return column.unsqueeze(2).broadcast_to([P, NB, D])


def layernorm_stats(V, own, ln, s_var):
    own.link(V.tensor_reduce(ln.total[:], ln.h[:], AX.X, ALU.add))
    own.link(V.tensor_scalar(ln.mean[:], ln.total[:], 1.0 / D, None, ALU.mult))
    own.link(V.tensor_tensor(ln.centred[:], ln.h[:], over_tokens(ln.mean[:]), ALU.subtract))
    own.link(V.tensor_tensor(ln.square[:], ln.centred[:], ln.centred[:], ALU.mult))
    own.link(V.tensor_reduce(ln.squares[:], ln.square[:], AX.X, ALU.add))
    V.tensor_scalar(ln.var[:], ln.squares[:], 1.0 / D, EPS, ALU.mult, ALU.add).then_inc(s_var, 1)


def layernorm_norm(V, own, ln, s_n):
    own.link(V.reciprocal(ln.r0[:], ln.dev[:]))
    own.link(V.tensor_tensor(ln.t1[:], ln.r0[:], ln.r0[:], ALU.mult))
    own.link(V.tensor_tensor(ln.t2[:], ln.t1[:], ln.var[:], ALU.mult))
    own.link(V.tensor_scalar(ln.t3[:], ln.t2[:], -0.5 * X_SCALE, 1.5 * X_SCALE, ALU.mult, ALU.add))
    own.link(V.tensor_tensor(ln.r[:], ln.r0[:], ln.t3[:], ALU.mult))
    own.link(V.tensor_tensor(ln.square[:], ln.centred[:], over_tokens(ln.r[:]), ALU.mult))
    own.link(V.tensor_copy(ln.split[:, :, 0:D], ln.square[:]))
    V.tensor_tensor(ln.split[:, :, D:2 * D], ln.square[:], ln.split[:, :, 0:D], ALU.subtract).then_inc(s_n, 1)


def token_mixing(nc, m):
    a = m.a
    ctx, sb, sem = tools(nc)
    NT = 2 * NB
    PREP = 6
    LINKS = LN_LINKS + 1
    with ctx:
        x_rows = [sb(f"x_rows{k}", [P, NB, D], F32) for k in range(2)]
        xT = [sb(f"xT{k}", [D + 1, T], F32) for k in range(2)]
        qT = [sb(f"qT{k}", [D, T], F32) for k in range(2)]
        kT = [sb(f"kT{k}", [D, T], F32) for k in range(2)]
        vo = [sb(f"vo{k}", [P, NB, D], F32) for k in range(2)]
        yT = [sb(f"yT{k}", [P, HALF], F32) for k in range(2)]
        gated = sb("gated", [P, 2, HALF], F32)
        neg = sb("neg", [P, NB, D], F32)
        hello = sb("hello", [P, 4], F32)
        ln = Layernorm(sb, "tok_ln_")
        s_x = [sem(f"x_loaded{k}") for k in range(2)]
        s_prep, s_kept, s_s, s_g, s_av, s_yT = (sem(n) for n in (
            "prep_tile_made", "prep_tile_kept", "scores_made", "scores_gated", "products_made",
            "yT_kept"))
        s_y, s_h, s_hk, s_own, s_var, s_sd, s_n, s_nT, s_nk, s_set = (sem(n) for n in (
            "y_turned", "h_made", "h_kept", "tok_dve_step", "variance_made", "deviation_made", "normed_made",
            "normed_turned", "normed_kept", "ones_set"))

        with nc.Block() as block:
            @block.sync
            def _(sp):
                for k in range(2):
                    sp.dma_start(x_rows[k][:], a["x"][k, 0].rearrange("(c p) d -> p c d", p=P)).then_inc(s_x[k], 16)
                with sp.Fori(0, B // 2 - 1) as i:
                    for k in range(2):
                        sp.wait_ge(s_prep, 2 * PREP * i + PREP * k + 1)
                        sp.dma_start(x_rows[k][:], a["x"][2 * i + 2 + k, 0].rearrange("(c p) d -> p c d", p=P)
                                     ).then_inc(s_x[k], 16)

            @block.tensor
            def _(pe):
                bank, mm = m.bank, nc.tensor.matmul
                pe.wait_ge(s_set, 3)
                with pe.Fori(0, B // 2) as i:
                    def prep(k):
                        n = 2 * PREP * i + PREP * k
                        pe.wait_ge(s_x[k], 16 * i + 16)
                        for tile in range(PREP):
                            z = bank[5 + tile % 2]
                            pe.wait_ge(s_kept, n + tile + 1)
                            if tile == 1:
                                pe.wait_ge(s_kept, n + 3)
                            for c in range(4 if tile == 0 else NB if tile == 5 else 1):
                                if tile == 0:
                                    last = nc.tensor.transpose(
                                        z[:, c * P:(c + 1) * P],
                                        x_rows[k][:, 2 * c:2 * c + 2, :].rearrange("p c d -> p (c d)"), m.ident[:])
                                elif tile < 5:
                                    half = (tile + 1) % 2
                                    last = mm(z[0:D, :], (m.wq if tile < 3 else m.wk)[:],
                                              xT[k][:, half * HALF:(half + 1) * HALF], start=True, stop=True)
                                else:
                                    last = mm(z[:, c * D:(c + 1) * D], xT[k][:, c * P:(c + 1) * P], m.wvo[:],
                                              start=(c == 0), stop=True, skip_group_check=True)
                            last.then_inc(s_prep, 1)

                    def scores(k, t):
                        half, s = divmod(t, NB)
                        pe.wait_ge(s_g, 2 * NT * i + NT * k + t + 1)
                        mm(bank[t % 2][:], kT[k][:, s * P:(s + 1) * P], qT[k][:, half * HALF:(half + 1) * HALF],
                           start=True, stop=True).then_inc(s_s, 1)

                    def product(k, t):
                        half, s = divmod(t, NB)
                        if t == 0:
                            pe.wait_ge(s_yT, 2 * i + k + 1)
                        pe.wait_ge(s_g, 2 * NT * i + NT * k + t + 3)
                        mm(bank[3 + k][half * D:(half + 1) * D, :], vo[k][:, s, :], gated[:, t % 2, :],
                           start=(s == 0), stop=(s == NB - 1)).then_inc(s_av, 1)

                    def turn_y(k):
                        pe.wait_ge(s_nk, 2 * i + k + 1)
                        pe.wait_ge(s_yT, 2 * i + k + 3)
                        for c in range(4):
                            last = nc.tensor.transpose(bank[7][:, c * P:(c + 1) * P], yT[k][:, c * P:(c + 1) * P],
                                                       m.ident[:])
                        last.then_inc(s_y, 1)

                    def turn_normed(k):
                        pe.wait_ge(s_n, 2 * i + k + 1)
                        for q in range(NB):
                            t = TOKENS_OF[q] * P
                            last = nc.tensor.transpose(bank[7][:].bitcast(F16)[:, t:t + P],
                                                       ln.split[:, q, :], m.ident16[:])
                        last.then_inc(s_nT, 1)

                    for k in range(2):
                        prep(k)
                    pe.wait_ge(s_kept, 2 * PREP * i + 2 * PREP + 2)
                    for k in range(2):
                        scores(k, 0)
                        for t in range(NT):
                            if t + 1 < NT:
                                scores(k, t + 1)
                            product(k, t)
                            if k == 1 and t == 2:
                                turn_y(0)
                            if k == 1 and t == 12:
                                turn_normed(0)
                    turn_y(1)
                    turn_normed(1)

            @block.scalar
            def _(act):
                S = nc.scalar
                S.activation(hello[:, 0:1], m.ident[:, 0:1], ACT.Sqrt).then_inc(s_set, 1)
                act.wait_ge(s_set, 3)
                for n, (s, free) in enumerate(((s_kept, 2), (s_yT, 2), (s_nk, 1), (s_hk, 1))):
                    S.copy(hello[:, n:n + 1], m.ident[:, 0:1]).then_inc(s, free)
                with act.Fori(0, B // 2) as i:
                    def keep_yT(k):
                        act.wait_ge(s_av, 2 * NT * i + NT * (k + 1))
                        S.activation(yT[k][:], m.bank[3 + k][:], ACT.Identity, bias=m.bo_col[:, 0:1]).then_inc(s_yT, 1)

                    def rest(k):
                        act.wait_ge(s_h, 2 * i + k + 1)
                        S.copy(m.res[:, 2 * i + k, :, :], ln.h[:]).then_inc(s_hk, 1)
                        act.wait_ge(s_var, 2 * i + k + 1)
                        S.activation(ln.dev[:], ln.var[:], ACT.Sqrt).then_inc(s_sd, 1)
                        act.wait_ge(s_nT, 2 * i + k + 1)
                        S.copy(m.xs[:, COLS:COLS + T * B].rearrange("p (t b) -> p t b", b=B)[:, :, 2 * i + k],
                               m.bank[7][:].bitcast(F16)).then_inc(s_nk, 1)

                    for k in range(2):
                        for tile in range(PREP):
                            act.wait_ge(s_prep, 2 * PREP * i + PREP * k + tile + 1)
                            z = m.bank[5 + tile % 2]
                            if tile == 0:
                                pairs = xT[k][0:D, :].rearrange("d (c two j) -> d c two j", two=2, j=P)
                                S.copy(pairs[:, :, 0, :], z[0:D, :].rearrange("d (c j) -> d c j", j=P))
                                last = S.copy(pairs[:, :, 1, :], z[D:P, :].rearrange("d (c j) -> d c j", j=P))
                            elif tile < 5:
                                half = (tile + 1) % 2
                                last = S.copy((qT, kT)[(tile - 1) // 2][k][:, half * HALF:(half + 1) * HALF], z[0:D, :])
                            else:
                                last = S.copy(vo[k][:].rearrange("p c d -> p (c d)"), z[:])
                            last.then_inc(s_kept, 1)
                    for k in range(2):
                        keep_yT(k)
                        rest(k)

            @block.vector
            def _(dve):
                V = nc.vector
                for k in range(2):
                    V.memset(xT[k][D:D + 1, :], 1.0).then_inc(s_set, 1)
                V.memset(neg[:, 0, 0:1], 0.0).then_inc(s_g, 2)
                dve.wait_ge(s_g, 2)
                with dve.Fori(0, B // 2) as i:
                    own = Links(dve, s_own, 2 * LINKS * i)

                    def gate(k, t):
                        half, s = divmod(t, NB)
                        dve.wait_ge(s_s, 2 * NT * i + NT * k + t + 1)
                        V.tensor_tensor(gated[:, t % 2, :], m.bank[t % 2][:],
                                        m.gT[:, s, half * HALF:(half + 1) * HALF], ALU.mult).then_inc(s_g, 1)

                    def prelu(k):
                        dve.wait_ge(s_y, 2 * i + k + 1)
                        dve.wait_ge(s_hk, 2 * i + k + 1)
                        y = m.bank[7][:].rearrange("p (c d) -> p c d", d=D)
                        own.link(V.tensor_scalar(neg[:], y, 0.0, m.a_col[:, 0:1], ALU.min, ALU.mult))
                        V.scalar_tensor_tensor(ln.h[:], y, 0.0, neg[:], ALU.max, ALU.add).then_inc(s_h, 1)
                        dve.wait_ge(s_h, 2 * i + k + 1)

                    def norm(k):
                        dve.wait_ge(s_sd, 2 * i + k + 1)
                        layernorm_norm(V, own, ln, s_n)

                    for t in range(NT):
                        gate(0, t)
                    for t in range(NT):
                        gate(1, t)
                        if t == 3:
                            prelu(0)
                        if t == 5:
                            layernorm_stats(V, own, ln, s_var)
                        if t == 8:
                            norm(0)
                    prelu(1)
                    layernorm_stats(V, own, ln, s_var)
                    norm(1)
                    assert own.n == 2 * LINKS, own.n


class Chain:

    def __init__(self, sb, sem, d, name):
        self.d = d
        self.tanh = sb(f"tanh_gates_{name}", [P, 4, B], F32)
        self.cell, self.forgot, self.added, self.out_gate, self.tanh_cell, self.h = (
            sb(f"{part}_{name}", [P, B], F32) for part in ("cell", "forgot", "added", "out_gate", "tanh_cell", "h"))
        (self.s_z_fg, self.s_z_io, self.s_t_fg, self.s_t_io, self.s_added, self.s_cell, self.s_tanh_cell,
         self.s_hi, self.s_h, self.s_lo) = (sem(f"{s}_{name}") for s in (
             "z_fg", "z_io", "t_fg", "t_io", "added", "cell", "tanh_cell", "hi", "h", "lo"))



def pe_gates(nc, pe, m, c, n, h_hi, h_lo, fg, io):
    z = (fg[:, 0, :], fg[:, 1, :], io[:, 0, :], io[:, 1, :])
    pe.wait_ge(c.s_hi, n + 1)
    for w in (m.u_lo[c.d], m.u_hi[c.d]):
        for g in range(4):
            nc.tensor.matmul(z[g], w[:, g, :], h_hi, start=False, stop=False, skip_group_check=True)
    pe.wait_ge(c.s_lo, n + 1)
    for g in range(4):
        last = nc.tensor.matmul(z[g], m.u_hi[c.d][:, g, :], h_lo, start=False, stop=True, skip_group_check=True)
        if g == G_:
            last.then_inc(c.s_z_fg, 1)
    last.then_inc(c.s_z_io, 1)


def act_gates(nc, act, c, n, fg, io):
    act.wait_ge(c.s_z_fg, n + 1)
    nc.scalar.activation(c.tanh[:, 0:2, :], fg, ACT.Tanh, scale=1.0 / Z_SCALE).then_inc(c.s_t_fg, 1)
    act.wait_ge(c.s_z_io, n + 1)
    nc.scalar.activation(c.tanh[:, 2:4, :], io, ACT.Tanh, scale=1.0 / Z_SCALE).then_inc(c.s_t_io, 1)


def act_cell(nc, act, c, n):
    act.wait_ge(c.s_cell, n + 1)
    nc.scalar.activation(c.tanh_cell[:], c.cell[:], ACT.Tanh, scale=0.5).then_inc(c.s_tanh_cell, 1)


def dve_terms(nc, dve, c, n):
    stt = nc.vector.scalar_tensor_tensor
    dve.wait_ge(c.s_t_fg, n + 1)
    stt(c.forgot[:], c.tanh[:, F_, :], 1.0, c.cell[:], ALU.add, ALU.mult)
    dve.wait_ge(c.s_t_io, n + 1)
    stt(c.added[:], c.tanh[:, I_, :], 1.0, c.tanh[:, G_, :], ALU.add, ALU.mult).then_inc(c.s_added, 1)


def dve_cell(nc, dve, c, n):
    nc.vector.tensor_scalar(c.out_gate[:], c.tanh[:, O_, :], 1.0, 0.5 * X_SCALE, ALU.add, ALU.mult)
    dve.wait_ge(c.s_added, n + 1)
    nc.vector.scalar_tensor_tensor(c.cell[:], c.forgot[:], 0.5, c.added[:], ALU.mult, ALU.add).then_inc(c.s_cell, 1)


def dve_hidden(nc, dve, c, n, h_hi):
    tt = nc.vector.tensor_tensor
    dve.wait_ge(c.s_tanh_cell, n + 1)
    tt(h_hi, c.out_gate[:], c.tanh_cell[:], ALU.mult).then_inc(c.s_hi, 1)
    tt(c.h[:], c.out_gate[:], c.tanh_cell[:], ALU.mult).then_inc(c.s_h, 1)


def dve_hidden_low(nc, dve, c, n, h_hi, h_lo):
    dve.wait_ge(c.s_h, n + 1)
    nc.vector.tensor_tensor(h_lo, c.h[:], h_hi, ALU.subtract).then_inc(c.s_lo, 1)


def encoder(nc, m):
    ctx, sb, sem = tools(nc)
    with ctx:
        ch = [Chain(sb, sem, d, name) for d, name in enumerate(("fwd", "bwd"))]
        s_set = sem("encoder_state_set")
        hello = sb("encoder_hello", [P, 1], F32)
        h = list(zip(m.enc_hi, m.enc_lo))

        banks = [[[m.bank[4 * d + 2 * p + j][:].rearrange("p (g t b) -> p g t b", g=2, t=CH) for j in range(2)]
                  for p in range(2)] for d in range(2)]

        def at(d, step):
            p, s = divmod(step, CH)
            s = CH - 1 - s if d else s
            return [z[:, :, s, :] for z in banks[d][p]]

        with nc.Block() as block:
            @block.tensor
            def _(pe):
                def fill(d, p, unit, col):
                    g, half = divmod(unit, 2)
                    z = banks[d][p][g // 2][:, g % 2, half * CH // 2:(half + 1) * CH // 2, :]
                    nc.tensor.matmul(z, m.w_hi[d][:, g, :], m.xs[:, bass.ds(col, HALFCH)],
                                     start=(unit % 4 == 0), stop=False, skip_group_check=True)
                    nc.tensor.matmul(z, m.w_lo[d][:, g, :], m.xs[:, bass.ds(col, HALFCH)],
                                     start=False, stop=False, skip_group_check=True)
                    nc.tensor.matmul(z, m.lstm_bias[d][:, g, :], m.ones3[:],
                                     start=False, stop=False, skip_group_check=True)

                for d in range(2):
                    for unit in range(8):
                        fill(d, 0, unit, COLS + (NCH - 1) * COLS * d + (unit % 2) * HALFCH)
                with pe.Fori(0, NCH // 2) as i:
                    for step in range(2 * CH):
                        p, s = divmod(step, CH)
                        for d in range(2):
                            fg, io = at(d, step)
                            pe_gates(nc, pe, m, ch[d], 2 * CH * i + step, h[d][0][:], h[d][1][:], fg, io)
                            if s % 2 == d:
                                unit = s // 2
                                col = (unit % 2) * HALFCH + (COLS * (NCH - 1 - p) - 2 * COLS * i if d else
                                                            COLS * (2 + p) + 2 * COLS * i)
                                fill(d, 1 - p, unit, col)

            @block.scalar
            def _(act):
                nc.scalar.activation(hello[:], m.ident[:, 0:1], ACT.Gelu)
                with act.Fori(0, NCH // 2) as i:
                    for step in range(2 * CH):
                        n = 2 * CH * i + step
                        act_cell(nc, act, ch[1], n)
                        act_gates(nc, act, ch[0], n, *at(0, step))
                        act_cell(nc, act, ch[0], n)
                        act_gates(nc, act, ch[1], n, *at(1, step))
                act_cell(nc, act, ch[1], T)

            @block.vector
            def _(dve):
                own = Links(dve, s_set)
                for d in range(2):
                    own.link(nc.vector.memset(ch[d].cell[:], 0.0))
                    own.link(nc.vector.memset(ch[d].out_gate[:], 0.0))
                nc.vector.memset(h[0][0][:], 0.0).then_inc(ch[0].s_hi, 1)
                nc.vector.memset(h[0][1][:], 0.0).then_inc(ch[0].s_lo, 1)
                nc.vector.memset(ch[1].cell[:], 0.0).then_inc(ch[1].s_cell, 1)
                with dve.Fori(0, NCH // 2) as i:
                    for step in range(2 * CH):
                        n = 2 * CH * i + step
                        for d in range(2):
                            late = 1 - d
                            dve_hidden(nc, dve, ch[late], n, h[late][0][:])
                            dve_terms(nc, dve, ch[d], n)
                            dve_hidden_low(nc, dve, ch[late], n, h[late][0][:], h[late][1][:])
                            dve_cell(nc, dve, ch[d], n)
                dve_hidden(nc, dve, ch[1], T, h[1][0][:])
                dve_hidden_low(nc, dve, ch[1], T, h[1][0][:], h[1][1][:])


def decoder(nc, m):
    ctx, sb, sem = tools(nc)
    with ctx:
        c = Chain(sb, sem, 2, "dec")
        ring_hi = sb("ring_hi", [P, 2 * CH, B], F16)
        ring_lo = sb("ring_lo", [P, 2 * CH, B], F16)
        given = sb("given", [P, 4 * B], F32)
        left = sb("given_left", [P, 2, 4 * B], F32)
        parts = sb("given_parts", [P, 3, 4, B], BF16)
        s_copied = [sem(f"h_chunk_copied{p}") for p in range(2)]
        s_given, s_parts, s_set = (sem(n) for n in ("given_made", "given_split", "decoder_set"))
        banks = [[m.bank[2 * p + j][:].rearrange("p (g t b) -> p g t b", g=2, t=CH) for j in range(2)]
                 for p in range(2)]

        def at(step):
            p, s = divmod(step, CH)
            return [z[:, :, s, :] for z in banks[p]]

        with nc.Block() as block:
            @block.sync
            def _(sp):
                with sp.Fori(0, NCH // 2) as i:
                    for p in range(2):
                        sp.wait_ge(c.s_lo, 2 * CH * i + CH * (p + 1) + 1)
                        for ring, all_h in ((ring_hi, m.dec_hi), (ring_lo, m.dec_lo)):
                            sp.dma_start(all_h[:, bass.ds((2 * i + p) * COLS, COLS)],
                                         ring[:, p * CH:(p + 1) * CH, :].rearrange("p t b -> p (t b)")
                                         ).then_inc(s_copied[p], 16)
                for p in range(2):
                    sp.wait_ge(s_copied[p], 16 * NCH + 1)

            @block.tensor
            def _(pe):
                def fill(p, unit):
                    g, half = divmod(unit, 2)
                    z = banks[p][g // 2][:, g % 2, half * CH // 2:(half + 1) * CH // 2, :]
                    for k in range(3):
                        nc.tensor.matmul(z, m.identb[:], parts[:, k, g, :].unsqueeze(1).broadcast_to([P, CH // 2, B]),
                                         start=(unit % 4 == 0 and k == 0), stop=False, skip_group_check=True)

                z = m.bank[4][:, 0:4 * B]
                for g in range(4):
                    zg = z[:, g * B:(g + 1) * B]
                    for d in range(2):
                        for w, v in ((m.wd_hi, m.enc_hi), (m.wd_lo, m.enc_hi), (m.wd_hi, m.enc_lo)):
                            nc.tensor.matmul(zg, w[d][:, g, :], v[d][:], start=(g == 0 and d == 0 and v is m.enc_hi and w is m.wd_hi),
                                             stop=False, skip_group_check=True)
                    last = nc.tensor.matmul(zg, m.lstm_bias[2][:, g, :], m.ones3[:, 0:B], start=False, stop=True,
                                            skip_group_check=True)
                last.then_inc(s_given, 1)
                pe.wait_ge(s_parts, 1)
                for unit in range(8):
                    fill(0, unit)
                with pe.Fori(0, NCH // 2) as i:
                    for step in range(2 * CH):
                        p, s = divmod(step, CH)
                        before = (step - 1) % (2 * CH)
                        pe_gates(nc, pe, m, c, 2 * CH * i + step, ring_hi[:, before, :], ring_lo[:, before, :], *at(step))
                        if s % 2 == 0:
                            fill(1 - p, s // 2)

            @block.scalar
            def _(act):
                with act.Fori(0, NCH // 2) as i:
                    for step in range(2 * CH):
                        n = 2 * CH * i + step
                        act_gates(nc, act, c, n, *at(step))
                        act_cell(nc, act, c, n)

            @block.vector
            def _(dve):
                V = nc.vector
                own = Links(dve, s_set)
                own.link(V.memset(c.cell[:], 0.0))
                V.memset(ring_hi[:, 2 * CH - 1, :], 0.0).then_inc(c.s_hi, 1)
                V.memset(ring_lo[:, 2 * CH - 1, :], 0.0).then_inc(c.s_lo, 1)
                for p in range(2):
                    V.memset(left[:, p], 0.0).then_inc(s_copied[p], 1)
                dve.wait_ge(s_copied[1], 1)
                dve.wait_ge(s_given, 1)
                own.link(V.tensor_copy(given[:], m.bank[4][:, 0:4 * B]))
                flat = parts[:].rearrange("p k g b -> p k (g b)")
                own.link(V.tensor_copy(flat[:, 0], given[:]))
                own.link(V.tensor_tensor(left[:, 0], given[:], flat[:, 0], ALU.subtract))
                own.link(V.tensor_copy(flat[:, 1], left[:, 0]))
                own.link(V.tensor_tensor(left[:, 1], left[:, 0], flat[:, 1], ALU.subtract))
                V.tensor_copy(flat[:, 2], left[:, 1]).then_inc(s_parts, 1)
                with dve.Fori(0, NCH // 2) as i:
                    for step in range(2 * CH):
                        n = 2 * CH * i + step
                        p, s = divmod(step, CH)
                        dve_terms(nc, dve, c, n)
                        dve_cell(nc, dve, c, n)
                        if s == 0:
                            dve.wait_ge(s_copied[p], 32 * i + 1)
                        dve_hidden(nc, dve, c, n, ring_hi[:, step, :])
                        dve_hidden_low(nc, dve, c, n, ring_hi[:, step, :], ring_lo[:, step, :])


def project_and_route(nc, m):
    ctx, sb, sem = tools(nc)
    ROUTE_LINKS = 13
    LINKS = LN_LINKS + ROUTE_LINKS
    with ctx:
        ln = Layernorm(sb, "route_ln_")
        hello = sb("route_hello", [P, 4], F32)
        rank = sb("rank", [P, E], F32)
        wide = {name: sb("route_" + name, [P, NB, E], F32)
                for name in ("score", "equal0", "ranked0", "first", "masked", "equal1", "ranked1", "second", "chosen")}
        best = [sb(f"best{k}", [P, NB], F32) for k in range(4)]
        s_d, s_h, s_hk, s_own, s_var, s_sd, s_n, s_nT, s_nk, s_s, s_m, s_rank = (sem(n) for n in (
            "projected", "route_h_made", "route_h_kept", "route_dve_step", "route_variance", "route_deviation",
            "route_normed", "route_turned", "route_kept", "gate_scores", "masks_made", "rank_made"))

        with nc.Block() as block:
            @block.gpsimd
            def _(pool):
                nc.gpsimd.iota(wide["chosen"][:, 0, :].bitcast(mybir.dt.int32), pattern=[[-1, E]], base=E,
                               channel_multiplier=0).then_inc(s_rank, 1)
                pool.wait_ge(s_rank, 1)
                nc.gpsimd.tensor_copy(rank[:], wide["chosen"][:, 0, :].bitcast(mybir.dt.int32)).then_inc(s_rank, 1)

            @block.tensor
            def _(pe):
                hi = m.dec_hi.rearrange("p (t b) -> p t b", b=B)
                lo = m.dec_lo.rearrange("p (t b) -> p t b", b=B)
                with pe.Fori(0, B) as i:
                    pe.wait_ge(s_hk, i + 1)
                    for q in range(NB):
                        t = TOKENS_OF[q] * P
                        z = m.bank[0][:, q * D:(q + 1) * D]
                        nc.tensor.matmul(z, m.ones3[:], m.wo_bias, start=(q == 0), stop=False, skip_group_check=True)
                        for h, wo in ((hi, m.wo_hi), (hi, m.wo_lo), (lo, m.wo_hi)):
                            last = nc.tensor.matmul(z, h[:, t:t + P, i], wo[:], start=False, stop=True,
                                                    skip_group_check=True)
                    last.then_inc(s_d, 1)
                    pe.wait_ge(s_n, i + 1)
                    for q in range(NB):
                        t = TOKENS_OF[q] * P
                        last = nc.tensor.transpose(m.bank[1][:].bitcast(F16)[:, t:t + P], ln.split[:, q, :], m.ident16[:])
                    last.then_inc(s_nT, 1)
                    pe.wait_ge(s_nk, i + 1)
                    for q in range(NB):
                        x = m.xn[:, bass.ds(i * T + TOKENS_OF[q] * P, P)]
                        z = m.bank[2][:, q * E:(q + 1) * E]
                        nc.tensor.matmul(z, m.ones3[:], m.gate_bias, start=(q == 0), stop=False, skip_group_check=True)
                        nc.tensor.matmul(z, x, m.wg_hi[:], start=False, stop=False, skip_group_check=True)
                        last = nc.tensor.matmul(z, x, m.wg_lo[:], start=False, stop=True, skip_group_check=True)
                    last.then_inc(s_s, 1)

            @block.scalar
            def _(act):
                S = nc.scalar
                S.activation(hello[:, 0:1], m.ident[:, 0:1], ACT.Sqrt).then_inc(s_hk, 1)
                act.wait_ge(s_hk, 1)
                with act.Fori(0, B) as i:
                    act.wait_ge(s_h, i + 1)
                    S.copy(m.res[:, i, :, :], ln.h[:]).then_inc(s_hk, 1)
                    act.wait_ge(s_var, i + 1)
                    S.activation(ln.dev[:], ln.var[:], ACT.Sqrt).then_inc(s_sd, 1)
                    act.wait_ge(s_nT, i + 1)
                    S.copy(m.xn[:, bass.ds(i * T, T)], m.bank[1][:].bitcast(F16)).then_inc(s_nk, 1)

            @block.vector
            def _(dve):
                V = nc.vector
                dve.wait_ge(s_rank, 2)
                ranks = rank[:].unsqueeze(1).broadcast_to([P, NB, E])
                each = lambda k: best[k][:].unsqueeze(2).broadcast_to([P, NB, E])
                with dve.Fori(0, B) as i:
                    own = Links(dve, s_own, LINKS * i)
                    dve.wait_ge(s_d, i + 1)
                    dve.wait_ge(s_hk, i + 1)
                    V.scalar_tensor_tensor(ln.h[:], m.bank[0][:].rearrange("p (q d) -> p q d", d=D), 1.0 / Z_SCALE,
                                           m.res[:, i, :, :], ALU.mult, ALU.add).then_inc(s_h, 1)
                    dve.wait_ge(s_h, i + 1)
                    layernorm_stats(V, own, ln, s_var)
                    dve.wait_ge(s_sd, i + 1)
                    layernorm_norm(V, own, ln, s_n)
                    dve.wait_ge(s_s, i + 1)
                    own.link(V.tensor_scalar(wide["score"][:], m.bank[2][:, 0:NB * E].rearrange("p (q e) -> p q e", e=E),
                                             1.0 / Z_SCALE, None, ALU.mult))
                    for score, equal, ranked, top, first, k in ((wide["score"], wide["equal0"], wide["ranked0"], wide["first"], True, 0),
                                                                (wide["masked"], wide["equal1"], wide["ranked1"], wide["second"], False, 2)):
                        own.link(V.tensor_reduce(best[k][:], score[:], AX.X, ALU.max))
                        own.link(V.tensor_tensor(equal[:], score[:], each(k), ALU.is_equal))
                        own.link(V.tensor_tensor(ranked[:], equal[:], ranks, ALU.mult))
                        own.link(V.tensor_reduce(best[k + 1][:], ranked[:], AX.X, ALU.max))
                        own.link(V.tensor_tensor(top[:], ranked[:], each(k + 1), ALU.is_equal))
                        if first:
                            own.link(V.scalar_tensor_tensor(wide["masked"][:], wide["first"][:], -3e38, wide["score"][:], ALU.mult, ALU.add))
                    own.link(V.tensor_tensor(wide["chosen"][:], wide["first"][:], wide["second"][:], ALU.add))
                    V.tensor_scalar(m.mask[:, i, :, 0:E], wide["chosen"][:], -1.0, None, ALU.add)
                    V.tensor_copy(m.mask[:, i, :, E:2 * E], wide["chosen"][:]).then_inc(s_m, 1)
                    dve.wait_ge(s_m, i + 1)
                    assert own.n == LINKS, own.n


def experts(nc, m):
    ctx, sb, sem = tools(nc)
    with ctx:
        NT = 2 * E
        mask_now = sb("mask_now", [P, NB, 2 * E], BF16)
        maskT = sb("maskT", [2 * E, T], BF16)
        hid = sb("hid", [HE, 4, HALF], F32)
        yT = [sb(f"ff_yT{k}", [D, HALF], F32) for k in range(2)]
        sums = [sb(f"sums{k}", [P, 4, D], F32) for k in range(2)]
        hello = sb("ff_hello", [P, 4], F32)
        free_set = sb("ff_free_set", [P, 5], F32)
        s_mn, s_mT, s_mk, s_pre, s_hid, s_ff, s_y, s_yT, s_yt, s_o = (sem(n) for n in (
            "mask_copied", "mask_turned", "maskT_kept", "pre_made", "hid_made", "hid_used", "ff_y_made",
            "ff_yT_kept", "ff_y_turned", "sum_made"))
        s_out = [sem(f"sum_stored{k}") for k in range(2)]

        with nc.Block() as block:
            @block.sync
            def _(sp):
                with sp.Fori(0, B) as i:
                    for k in range(2):
                        sp.wait_ge(s_o, 2 * i + k + 2)
                        sp.dma_start(m.out[i].rearrange("(c p) d -> p c d", p=P)[:, 4 * k:4 * k + 4, :],
                                     sums[k][:]).then_inc(s_out[k], 16)
                for k in range(2):
                    sp.wait_ge(s_out[k], 16 * B + 1)

            @block.tensor
            def _(pe):
                bank, mm = m.bank, nc.tensor.matmul
                with pe.Fori(0, B) as i:
                    pe.wait_ge(s_mn, i + 1)
                    pe.wait_ge(s_mk, i + 1)
                    for c in range(NB):
                        last = nc.tensor.transpose(bank[5][:].bitcast(BF16)[0:2 * E, c * P:(c + 1) * P],
                                                   mask_now[:, MASK_OF[c], :], m.identb[:])
                    last.then_inc(s_mT, 1)
                    pe.wait_ge(s_mk, i + 2)

                    def pre(t):
                        k, e = divmod(t, E)
                        pe.wait_ge(s_hid, NT * i + t + 1)
                        z = bank[t % 2][:]
                        x = m.xn[:, bass.ds(i * T + k * HALF, HALF)]
                        mm(z, m.w1_hi[:, e, :], x, start=True, stop=False)
                        mm(z, m.w1_lo[:, e, :], x, start=False, stop=False)
                        mm(z, m.pick[:, e, :], maskT[:, k * HALF:(k + 1) * HALF], start=False, stop=True
                           ).then_inc(s_pre, 1)

                    def post(t):
                        k, e = divmod(t, E)
                        y = bank[3 + k][0:D, :]
                        if e == 0:
                            pe.wait_ge(s_yT, 2 * i + k + 1)
                            for part in range(3):
                                mm(y, m.b2[:, part, :], maskT[:, k * HALF:(k + 1) * HALF], start=(part == 0),
                                   stop=False)
                        pe.wait_ge(s_hid, NT * i + t + 3)
                        last = mm(y, m.w2[:, e, :], hid[:, t % 4, :], start=False, stop=(e == E - 1))
                        last.then_inc(s_ff, 1)

                    def turn(k):
                        pe.wait_ge(s_o, 2 * i + k + 1)
                        pe.wait_ge(s_yT, 2 * i + k + 3)
                        for c in range(4):
                            last = mm(bank[6][:, c * D:(c + 1) * D], yT[k][:, c * P:(c + 1) * P], m.ident[0:D, 0:D],
                                      start=(c == 0), stop=True, skip_group_check=True)
                        last.then_inc(s_yt, 1)

                    pre(0)
                    for t in range(NT):
                        if t + 1 < NT:
                            pre(t + 1)
                        post(t)
                        if t == E + 2:
                            turn(0)
                    turn(1)

            @block.scalar
            def _(act):
                S = nc.scalar
                S.activation(hello[:, 0:1], m.ident[:, 0:1], ACT.Gelu).then_inc(s_hid, 2)
                act.wait_ge(s_hid, 2)
                with act.Fori(0, B) as i:
                    for t in range(NT):
                        act.wait_ge(s_pre, NT * i + t + 1)
                        S.activation(hid[:, t % 4, :], m.bank[t % 2][:], ACT.Gelu, scale=1.0 / Z_SCALE,
                                     bias=m.b1[:, t % E:t % E + 1]).then_inc(s_hid, 1)

            @block.vector
            def _(dve):
                V = nc.vector
                for n, (s, free) in enumerate(((s_mk, 1), (s_yT, 2), (s_o, 1), (s_out[0], 1), (s_out[1], 1))):
                    V.memset(free_set[:, n:n + 1], 0.0).then_inc(s, free)
                with dve.Fori(0, B) as i:
                    V.tensor_copy(mask_now[:], m.mask[:, i, :, :]).then_inc(s_mn, 1)
                    dve.wait_ge(s_mT, i + 1)
                    V.tensor_copy(maskT[:], m.bank[5][:].bitcast(BF16)[0:2 * E, :]).then_inc(s_mk, 1)
                    for k in range(2):
                        dve.wait_ge(s_ff, NT * i + E * (k + 1))
                        V.tensor_copy(yT[k][:], m.bank[3 + k][0:D, :]).then_inc(s_yT, 1)
                        dve.wait_ge(s_yt, 2 * i + k + 1)
                        dve.wait_ge(s_out[k], 16 * i + 1)
                        V.tensor_tensor(sums[k][:], m.bank[6][:, 0:4 * D].rearrange("p (c d) -> p c d", d=D),
                                        m.res[:, i, :, :].rearrange("p (c two) d -> p two c d", two=2)[:, k], ALU.add
                                        ).then_inc(s_o, 1)


def kernel(**inputs):
    import numpy as _np
    import concourse.bacc as _bacc
    from concourse import mybir as _mybir
    from concourse.bass_utils import run_bass_kernel_spmd as _run

    nc = _bacc.Bacc("TRN2", target_bir_lowering=False, num_devices=1)
    arrays, args = {}, {}
    for name in sorted(inputs):
        array = _np.ascontiguousarray(inputs[name])
        arrays[f"in_{name}_dram"] = array
        args[name] = nc.dram_tensor(f"in_{name}_dram", array.shape, _mybir.dt.from_np(array.dtype),
                                    kind="ExternalInput").ap()
    out = nc.dram_tensor("out_dram", (B, T, D), _mybir.dt.float32, kind="ExternalOutput").ap()
    build(nc, args, out)
    r = _run(nc, [arrays], core_ids=[0])
    return r.results[0]["out_dram"]
```

```python
from contextlib import ExitStack

import numpy as np
import concourse.bass as bass
from concourse import mybir

F32, F16, BF16 = mybir.dt.float32, mybir.dt.float16, mybir.dt.bfloat16
ALU = mybir.AluOpType
ACT = mybir.ActivationFunctionType
AX = mybir.AxisListType

P = 128
B, T, D = 16, 1024, 64
H = 128
E, HE = 8, 128
NB = T // P
HALF = 512
EPS = 1e-5

W_SCALE = 2.0 ** 6
X_SCALE = 2.0 ** 12
Z_SCALE = W_SCALE * X_SCALE
F_, G_, I_, O_ = range(4)
GATE_FROM = (1, 2, 0, 3)
GATE_SCALE = (0.5 * W_SCALE, W_SCALE, 0.5 * W_SCALE, 0.5 * W_SCALE)

CH = 16
COLS = CH * B
NCH = T // CH
HALFCH = COLS // 2
BIG = 2.0 ** 100


def tools(nc):
    ctx = ExitStack()
    return (ctx, lambda name, shape, dt: ctx.enter_context(nc.sbuf_tensor(name, shape, dt)),
            lambda name: ctx.enter_context(nc.semaphore(name)))


class Links:

    def __init__(self, engine, sem, base=0):
        self.engine, self.sem, self.base, self.n = engine, sem, base, 0

    def link(self, instruction):
        instruction.then_inc(self.sem, 1)
        self.n += 1
        self.engine.wait_ge(self.sem, self.base + self.n)


class Shared:
    pass


def build(nc, a, out):
    ctx = ExitStack()
    m = Shared()
    m.a, m.out = a, out

    def sb(name, shape, dt):
        return ctx.enter_context(nc.sbuf_tensor(name, shape, dt))

    with ctx:
        m.bank = [ctx.enter_context(nc.psum_tensor(f"bank{k}", [P, HALF], F32)) for k in range(8)]
        m.ident = sb("ident", [P, P], F32)
        m.ident16 = sb("ident16", [P, P], F16)
        m.identb = sb("identb", [P, P], BF16)
        m.kept = nc.dram_tensor("kept_h", (B, T, D), F32, kind="Internal").ap()
        m.gT = sb("gammaT", [P, NB, T], F32)
        m.xs = sb("xs", [P, T * B + 2 * COLS], F16)
        m.u_hi = [sb(f"u_hi{d}", [P, 4, H], F16) for d in range(3)]
        m.u_lo = [sb(f"u_lo{d}", [P, 4, H], F16) for d in range(3)]
        m.w_hi = [sb(f"w_hi{d}", [P, 4, H], F16) for d in range(2)]
        m.w_lo = [sb(f"w_lo{d}", [P, 4, H], F16) for d in range(2)]
        m.wd_hi = [sb(f"wd_hi{d}", [P, 4, H], F16) for d in range(2)]
        m.wd_lo = [sb(f"wd_lo{d}", [P, 4, H], F16) for d in range(2)]
        m.bias = sb("bias", [3, 3 * 4 * H + D + E], BF16)
        m.lstm_bias = [m.bias[:, 4 * H * d:4 * H * (d + 1)].rearrange("p (g h) -> p g h", g=4)
                       for d in range(3)]
        m.wo_bias = m.bias[:, 12 * H:12 * H + D]
        m.gate_bias = m.bias[:, 12 * H + D:12 * H + D + E]
        m.ones3 = sb("ones3", [3, P], BF16)
        m.a_col = sb("a_col", [P, 1], F32)
        m.bo_col = sb("bo_col", [P, 1], F32)
        m.wo_hi = sb("wo_hi", [P, D], F16)
        m.wo_lo = sb("wo_lo", [P, D], F16)
        m.wg_hi = sb("wg_hi", [P, E], F16)
        m.wg_lo = sb("wg_lo", [P, E], F16)
        m.w1_hi = sb("w1_hi", [P, E, HE], F16)
        m.w1_lo = sb("w1_lo", [P, E, HE], F16)
        m.w2 = sb("w2", [HE, E, D], F32)
        m.b1 = sb("b1", [HE, E], F32)
        m.b2 = sb("b2", [2 * E, 3, D], BF16)
        m.pick = sb("pick", [2 * E, E, HE], BF16)
        m.wq = sb("wq", [D + 1, D], F32)
        m.wk = sb("wk", [D + 1, D], F32)
        m.wvo = sb("wvo", [D + 1, D], F32)
        m.enc_hi = [sb(f"enc_hi{d}", [P, B], F16) for d in range(2)]
        m.enc_lo = [sb(f"enc_lo{d}", [P, B], F16) for d in range(2)]

        for phase in (setup, token_mixing, encoder, decoder_and_experts):
            phase(nc, m)


def setup(nc, m):
    a = m.a
    ctx, sb, sem = tools(nc)
    NBIAS = 12 * H + D + E
    with ctx:
        raw_u = [sb(f"raw_u{d}", [P, 4 * H], F32) for d in range(3)]
        raw_w = [sb(f"raw_w{d}", [P, 4 * H], F32) for d in range(2)]
        raw_wd = [sb(f"raw_wd{d}", [P, 4 * H], F32) for d in range(2)]
        raw_wo = sb("raw_wo", [P, D], F32)
        raw_wg = sb("raw_wg", [P, E], F32)
        raw_first = sb("raw_first", [P, E, HE], F32)
        raw_b = sb("raw_b", [3, NBIAS], F32)
        part = sb("part", [3, 3, NBIAS], BF16)
        left = sb("left", [3, 3, NBIAS], F32)
        raw_b2 = sb("raw_b2", [2 * E, 3, D], F32)
        wv = sb("wv", [D + 1, D], F32)
        tok_wo = sb("tok_wo", [D, D], F32)
        wvT = sb("wvT", [D, D + 1], F32)
        g_rows = [sb(f"g_rows{k}", [P, T], F32) for k in range(2)]
        s_w, s_b, s_dve, s_z, s_id, s_id0 = (sem(n) for n in
            ("weights_loaded", "vectors_loaded", "split_step", "b2_zeroed", "ident_made", "ident_zeroed"))
        s_g = [sem(f"gamma_loaded{k}") for k in range(2)]
        s_gt, s_gfree, s_v, s_vk = (sem(n) for n in
            ("gamma_turned", "gamma_banks_free", "wv_on_pe", "wv_kept"))
        n_w, n_b = [0], [0]


        with nc.Block() as block:
            @block.sync
            def _(sp):
                def load(dst, src, s=s_w, n=n_w, scattered=False):
                    sp.dma_start(dst, src, allow_slow_non_contiguous=scattered).then_inc(s, 16)
                    n[0] += 16

                for k in range(2):
                    sp.dma_start(g_rows[k][:], a["L0_tok_d_gamma_batched"][k * P:(k + 1) * P, :]).then_inc(s_g[k], 16)
                load(wv[0:D, :], a["L0_tok_Wv"])
                load(wv[D:D + 1, :], a["L0_tok_bv"][None, :])
                load(tok_wo[:], a["L0_tok_Wo"])
                load(m.wq[0:D, :], a["L0_tok_Wq"])
                load(m.wq[D:D + 1, :], a["L0_tok_bq"][None, :])
                load(m.wk[0:D, :], a["L0_tok_Wk"])
                load(m.wk[D:D + 1, :], a["L0_tok_bk"][None, :])
                for k in range(2):
                    load(m.bo_col[k * D:(k + 1) * D, :], a["L0_tok_bo"][:, None])
                load(m.a_col[:], a["L0_tok_prelu_a"][None, :].broadcast_to([P, 1]))
                for d, u in enumerate((a["L0_attn_Uf"], a["L0_attn_Ub"], a["L0_attn_Ud"])):
                    load(raw_u[d][:], u)
                for d, w in enumerate((a["L0_attn_Wf"], a["L0_attn_Wb"])):
                    load(raw_w[d][0:D, :], w)
                    load(raw_w[d][D:2 * D, :], w)
                for d in range(2):
                    load(raw_wd[d][:], a["L0_attn_Wd"][H * d:H * (d + 1), :])
                load(raw_wo[:], a["L0_attn_Wo"])
                for k in range(2):
                    load(raw_wg[k * D:(k + 1) * D, :], a["L0_ffn_Wg"])
                    load(raw_first[k * D:(k + 1) * D, :, :], a["L0_ffn_W1"].rearrange("e d h -> d e h"))
                load(m.w2[:], a["L0_ffn_W2"].rearrange("e h d -> h e d"))
                load(m.b1[:], a["L0_ffn_b1"].rearrange("e h -> h e"), scattered=True)
                for row in range(3):
                    for d, b in enumerate((a["L0_attn_bf"], a["L0_attn_bb"], a["L0_attn_bd"])):
                        for g in range(4):
                            k = (4 * d + g) * H
                            load(raw_b[row:row + 1, k:k + H],
                                 b[None, GATE_FROM[g] * H:(GATE_FROM[g] + 1) * H], s_b, n_b)
                    load(raw_b[row:row + 1, 12 * H:12 * H + D], a["L0_attn_bo"][None, :], s_b, n_b)
                    load(raw_b[row:row + 1, 12 * H + D:], a["L0_ffn_bg"][None, :], s_b, n_b)
                sp.wait_ge(s_z, 1)
                load(raw_b2[E:2 * E, 0, :], a["L0_ffn_b2"], s_b, n_b)
                with sp.Fori(0, NB // 2 - 1) as i:
                    for k in range(2):
                        sp.wait_ge(s_gt, 4 * i + 2 * k + 2)
                        sp.dma_start(g_rows[k][:], a["L0_tok_d_gamma_batched"][bass.ds((2 * i + k + 2) * P, P), :]
                                     ).then_inc(s_g[k], 16)

            @block.gpsimd
            def _(pool):
                nc.gpsimd.memset(m.ident[:], 0.0).then_inc(s_id0, 1)
                pool.wait_ge(s_id0, 1)
                nc.gpsimd.affine_select(out=m.ident[:], in_=m.ident[:], compare_op=ALU.not_equal, fill=1.0,
                                        base=0, pattern=[[-1, P]], channel_multiplier=1).then_inc(s_id, 1)
                nc.gpsimd.memset(raw_b2[:], 0.0).then_inc(s_z, 1)
                nc.gpsimd.memset(m.ones3[:], Z_SCALE)
                nc.gpsimd.memset(m.xs[:, 0:COLS], 0.0)
                nc.gpsimd.memset(m.xs[:, COLS + T * B:], 0.0)

            @block.tensor
            def _(pe):
                pe.wait_ge(s_id, 1)
                with pe.Fori(0, NB // 2) as i:
                    for k in range(2):
                        pe.wait_ge(s_g[k], 16 * i + 16)
                        for half in range(2):
                            pe.wait_ge(s_gfree, 4 * i + 2 * k + half + 1)
                            for s in range(4):
                                blk = 4 * half + s
                                last = nc.tensor.transpose(m.bank[2 * k + half][:, s * P:(s + 1) * P],
                                                           g_rows[k][:, blk * P:(blk + 1) * P], m.ident[:])
                            last.then_inc(s_gt, 1)
                pe.wait_ge(s_w, n_w[0])
                nc.tensor.transpose(m.bank[4][0:D, 0:D + 1], wv[:], m.ident[0:D + 1, 0:D + 1]).then_inc(s_v, 1)
                pe.wait_ge(s_vk, 1)
                nc.tensor.matmul(m.bank[5][0:D + 1, 0:D], wvT[:], tok_wo[:], start=True, stop=True).then_inc(s_v, 1)

            @block.scalar
            def _(act):
                act.wait_ge(s_id, 1)
                nc.scalar.copy(wvT[:], m.ident[0:D, 0:D + 1]).then_inc(s_gfree, 4)
                with act.Fori(0, NB // 2) as i:
                    for k in range(2):
                        for half in range(2):
                            act.wait_ge(s_gt, 4 * i + 2 * k + half + 1)
                            nc.scalar.copy(m.gT[:, 4 * half:4 * half + 4, bass.ds((2 * i + k) * P, P)],
                                           m.bank[2 * k + half][:].rearrange("p (s t) -> p s t", s=4)
                                           ).then_inc(s_gfree, 1)
                act.wait_ge(s_v, 1)
                nc.scalar.copy(wvT[:], m.bank[4][0:D, 0:D + 1]).then_inc(s_vk, 1)
                act.wait_ge(s_v, 2)
                nc.scalar.copy(m.wvo[:], m.bank[5][0:D + 1, 0:D])

            @block.vector
            def _(dve):
                own = Links(dve, s_dve)
                V = nc.vector
                dve.wait_ge(s_id, 1)
                V.tensor_copy(m.ident16[:], m.ident[:])
                V.tensor_copy(m.identb[:], m.ident[:])
                V.tensor_scalar(m.pick[:], m.ident[0:2 * E, 0:E].unsqueeze(2).broadcast_to([2 * E, E, HE]), BIG, None, ALU.mult)
                dve.wait_ge(s_w, n_w[0])

                def split(high, low, raw, scale):
                    own.link(V.tensor_scalar(high, raw, scale, None, ALU.mult))
                    V.scalar_tensor_tensor(low, raw, scale, high, ALU.mult, ALU.subtract)

                lstm = ([(m.u_hi[d], m.u_lo[d], raw_u[d]) for d in range(3)]
                        + [(m.w_hi[d], m.w_lo[d], raw_w[d]) for d in range(2)]
                        + [(m.wd_hi[d], m.wd_lo[d], raw_wd[d]) for d in range(2)])
                for high, low, raw in lstm:
                    for g in range(4):
                        k = GATE_FROM[g] * H
                        split(high[:, g, :], low[:, g, :], raw[:, k:k + H], GATE_SCALE[g])
                split(m.wo_hi[:], m.wo_lo[:], raw_wo[:], W_SCALE)
                split(m.wg_hi[:], m.wg_lo[:], raw_wg[:], W_SCALE)
                split(m.w1_hi[:], m.w1_lo[:], raw_first[:], W_SCALE)

                dve.wait_ge(s_b, n_b[0])
                for d in range(3):
                    for g in (F_, I_, O_):
                        k = (4 * d + g) * H
                        last = V.tensor_scalar(raw_b[:, k:k + H], raw_b[:, k:k + H], 0.5, None, ALU.mult)
                own.link(last)

                def thirds(value, part, left):
                    own.link(V.tensor_copy(part[:, 0], value))
                    own.link(V.tensor_tensor(left[:, 0], value, part[:, 0], ALU.subtract))
                    own.link(V.tensor_copy(part[:, 1], left[:, 0]))
                    own.link(V.tensor_tensor(left[:, 1], left[:, 0], part[:, 1], ALU.subtract))
                    own.link(V.tensor_copy(part[:, 2], left[:, 1]))

                thirds(raw_b[:], part, left)
                own.link(V.tensor_scalar(left[:, 0], part[:, 0], m.ident[0:3, 0:1], None, ALU.mult))
                own.link(V.scalar_tensor_tensor(left[:, 1], part[:, 1], m.ident[0:3, 1:2], left[:, 0],
                                                ALU.mult, ALU.add))
                V.scalar_tensor_tensor(m.bias[:], part[:, 2], m.ident[0:3, 2:3], left[:, 1], ALU.mult, ALU.add)
                thirds(raw_b2[:, 0, :], m.b2, raw_b2[:, 1:3, :])


TOKENS_OF = [4 * (q % 2) + q // 2 for q in range(NB)]
MASK_OF = [TOKENS_OF.index(c) for c in range(NB)]
LN_LINKS = 12


class Layernorm:

    def __init__(self, sb, name):
        one = lambda part: sb(name + part, [P, NB], F32)
        self.h, self.centred, self.square = (sb(name + part, [P, NB, D], F32) for part in ("h", "centred", "square"))
        self.split = sb(name + "split", [P, NB, 2 * D], F16)
        self.total, self.mean, self.squares, self.var, self.dev = (one(p) for p in
                                                                   ("total", "mean", "squares", "var", "dev"))
        self.r0, self.t1, self.t2, self.t3, self.r = (one(p) for p in ("r0", "t1", "t2", "t3", "r"))


def over_tokens(column):
    return column.unsqueeze(2).broadcast_to([P, NB, D])


def layernorm_stats(V, own, ln, s_var):
    own.link(V.tensor_reduce(ln.total[:], ln.h[:], AX.X, ALU.add))
    own.link(V.tensor_scalar(ln.mean[:], ln.total[:], 1.0 / D, None, ALU.mult))
    own.link(V.tensor_tensor(ln.centred[:], ln.h[:], over_tokens(ln.mean[:]), ALU.subtract))
    own.link(V.tensor_tensor(ln.square[:], ln.centred[:], ln.centred[:], ALU.mult))
    own.link(V.tensor_reduce(ln.squares[:], ln.square[:], AX.X, ALU.add))
    V.tensor_scalar(ln.var[:], ln.squares[:], 1.0 / D, EPS, ALU.mult, ALU.add).then_inc(s_var, 1)


def layernorm_norm(V, own, ln, s_n):
    own.link(V.reciprocal(ln.r0[:], ln.dev[:]))
    own.link(V.tensor_tensor(ln.t1[:], ln.r0[:], ln.r0[:], ALU.mult))
    own.link(V.tensor_tensor(ln.t2[:], ln.t1[:], ln.var[:], ALU.mult))
    own.link(V.tensor_scalar(ln.t3[:], ln.t2[:], -0.5 * X_SCALE, 1.5 * X_SCALE, ALU.mult, ALU.add))
    own.link(V.tensor_tensor(ln.r[:], ln.r0[:], ln.t3[:], ALU.mult))
    own.link(V.tensor_tensor(ln.square[:], ln.centred[:], over_tokens(ln.r[:]), ALU.mult))
    own.link(V.tensor_copy(ln.split[:, :, 0:D], ln.square[:]))
    V.tensor_tensor(ln.split[:, :, D:2 * D], ln.square[:], ln.split[:, :, 0:D], ALU.subtract).then_inc(s_n, 1)


def token_mixing(nc, m):
    a = m.a
    ctx, sb, sem = tools(nc)
    NT = 2 * NB
    PREP = 6
    LINKS = LN_LINKS + 1
    with ctx:
        x_rows = [sb(f"x_rows{k}", [P, NB, D], F32) for k in range(2)]
        xT = [sb(f"xT{k}", [D + 1, T], F32) for k in range(2)]
        qT = [sb(f"qT{k}", [D, T], F32) for k in range(2)]
        kT = [sb(f"kT{k}", [D, T], F32) for k in range(2)]
        vo = [sb(f"vo{k}", [P, NB, D], F32) for k in range(2)]
        yT = [sb(f"yT{k}", [P, HALF], F32) for k in range(2)]
        gated = sb("gated", [P, 2, HALF], F32)
        neg = sb("neg", [P, NB, D], F32)
        hello = sb("hello", [P, 4], F32)
        ln = Layernorm(sb, "tok_ln_")
        s_x = [sem(f"x_loaded{k}") for k in range(2)]
        s_prep, s_kept, s_s, s_g, s_av, s_yT = (sem(n) for n in (
            "prep_tile_made", "prep_tile_kept", "scores_made", "scores_gated", "products_made",
            "yT_kept"))
        s_y, s_h, s_hk, s_own, s_var, s_sd, s_n, s_nT, s_nk, s_set = (sem(n) for n in (
            "y_turned", "h_made", "h_kept", "tok_dve_step", "variance_made", "deviation_made", "normed_made",
            "normed_turned", "normed_kept", "ones_set"))

        with nc.Block() as block:
            @block.sync
            def _(sp):
                def store_h(b):
                    sp.wait_ge(s_h, b + 1)
                    for half in range(2):
                        sp.dma_start(m.kept[b].rearrange("(half c p) d -> p half c d", half=2, p=P)[:, half],
                                     ln.h[:].rearrange("p (c half) d -> p half c d", half=2)[:, half]).then_inc(s_hk, 16)

                for k in range(2):
                    sp.dma_start(x_rows[k][:], a["x"][k, 0].rearrange("(c p) d -> p c d", p=P)).then_inc(s_x[k], 16)
                with sp.Fori(0, B // 2 - 1) as i:
                    for k in range(2):
                        sp.wait_ge(s_prep, 2 * PREP * i + PREP * k + 1)
                        sp.dma_start(x_rows[k][:], a["x"][2 * i + 2 + k, 0].rearrange("(c p) d -> p c d", p=P)
                                     ).then_inc(s_x[k], 16)
                    for k in range(2):
                        store_h(2 * i + k)
                for b in range(B - 2, B):
                    store_h(b)
                sp.wait_ge(s_hk, 32 * B + 1)

            @block.tensor
            def _(pe):
                bank, mm = m.bank, nc.tensor.matmul
                pe.wait_ge(s_set, 3)
                with pe.Fori(0, B // 2) as i:
                    def prep(k):
                        n = 2 * PREP * i + PREP * k
                        pe.wait_ge(s_x[k], 16 * i + 16)
                        for tile in range(PREP):
                            z = bank[5 + tile % 2]
                            pe.wait_ge(s_kept, n + tile + 1)
                            if tile == 1:
                                pe.wait_ge(s_kept, n + 3)
                            for c in range(4 if tile == 0 else NB if tile == 5 else 1):
                                if tile == 0:
                                    last = nc.tensor.transpose(
                                        z[:, c * P:(c + 1) * P],
                                        x_rows[k][:, 2 * c:2 * c + 2, :].rearrange("p c d -> p (c d)"), m.ident[:])
                                elif tile < 5:
                                    half = (tile + 1) % 2
                                    last = mm(z[0:D, :], (m.wq if tile < 3 else m.wk)[:],
                                              xT[k][:, half * HALF:(half + 1) * HALF], start=True, stop=True)
                                else:
                                    last = mm(z[:, c * D:(c + 1) * D], xT[k][:, c * P:(c + 1) * P], m.wvo[:],
                                              start=(c == 0), stop=True, skip_group_check=True)
                            last.then_inc(s_prep, 1)

                    def scores(k, t):
                        half, s = divmod(t, NB)
                        pe.wait_ge(s_g, 2 * NT * i + NT * k + t + 1)
                        mm(bank[t % 2][:], kT[k][:, s * P:(s + 1) * P], qT[k][:, half * HALF:(half + 1) * HALF],
                           start=True, stop=True).then_inc(s_s, 1)

                    def product(k, t):
                        half, s = divmod(t, NB)
                        if t == 0:
                            pe.wait_ge(s_yT, 2 * i + k + 1)
                        pe.wait_ge(s_g, 2 * NT * i + NT * k + t + 3)
                        mm(bank[3 + k][half * D:(half + 1) * D, :], vo[k][:, s, :], gated[:, t % 2, :],
                           start=(s == 0), stop=(s == NB - 1)).then_inc(s_av, 1)

                    def turn_y(k):
                        pe.wait_ge(s_nk, 2 * i + k + 1)
                        pe.wait_ge(s_yT, 2 * i + k + 3)
                        for c in range(4):
                            last = nc.tensor.transpose(bank[7][:, c * P:(c + 1) * P], yT[k][:, c * P:(c + 1) * P],
                                                       m.ident[:])
                        last.then_inc(s_y, 1)

                    def turn_normed(k):
                        pe.wait_ge(s_n, 2 * i + k + 1)
                        for q in range(NB):
                            t = TOKENS_OF[q] * P
                            last = nc.tensor.transpose(bank[7][:].bitcast(F16)[:, t:t + P],
                                                       ln.split[:, q, :], m.ident16[:])
                        last.then_inc(s_nT, 1)

                    for k in range(2):
                        prep(k)
                    pe.wait_ge(s_kept, 2 * PREP * i + 2 * PREP + 2)
                    for k in range(2):
                        scores(k, 0)
                        for t in range(NT):
                            if t + 1 < NT:
                                scores(k, t + 1)
                            product(k, t)
                            if k == 1 and t == 2:
                                turn_y(0)
                            if k == 1 and t == 12:
                                turn_normed(0)
                    turn_y(1)
                    turn_normed(1)

            @block.scalar
            def _(act):
                S = nc.scalar
                S.activation(hello[:, 0:1], m.ident[:, 0:1], ACT.Sqrt).then_inc(s_set, 1)
                act.wait_ge(s_set, 3)
                for n, (s, free) in enumerate(((s_kept, 2), (s_yT, 2), (s_nk, 1), (s_hk, 1))):
                    S.copy(hello[:, n:n + 1], m.ident[:, 0:1]).then_inc(s, free)
                with act.Fori(0, B // 2) as i:
                    def keep_yT(k):
                        act.wait_ge(s_av, 2 * NT * i + NT * (k + 1))
                        S.activation(yT[k][:], m.bank[3 + k][:], ACT.Identity, bias=m.bo_col[:, 0:1]).then_inc(s_yT, 1)

                    def rest(k):
                        act.wait_ge(s_var, 2 * i + k + 1)
                        S.activation(ln.dev[:], ln.var[:], ACT.Sqrt).then_inc(s_sd, 1)
                        act.wait_ge(s_nT, 2 * i + k + 1)
                        S.copy(m.xs[:, COLS:COLS + T * B].rearrange("p (t b) -> p t b", b=B)[:, :, 2 * i + k],
                               m.bank[7][:].bitcast(F16)).then_inc(s_nk, 1)

                    for k in range(2):
                        for tile in range(PREP):
                            act.wait_ge(s_prep, 2 * PREP * i + PREP * k + tile + 1)
                            z = m.bank[5 + tile % 2]
                            if tile == 0:
                                pairs = xT[k][0:D, :].rearrange("d (c two j) -> d c two j", two=2, j=P)
                                S.copy(pairs[:, :, 0, :], z[0:D, :].rearrange("d (c j) -> d c j", j=P))
                                last = S.copy(pairs[:, :, 1, :], z[D:P, :].rearrange("d (c j) -> d c j", j=P))
                            elif tile < 5:
                                half = (tile + 1) % 2
                                last = S.copy((qT, kT)[(tile - 1) // 2][k][:, half * HALF:(half + 1) * HALF], z[0:D, :])
                            else:
                                last = S.copy(vo[k][:].rearrange("p c d -> p (c d)"), z[:])
                            last.then_inc(s_kept, 1)
                    for k in range(2):
                        keep_yT(k)
                        rest(k)

            @block.vector
            def _(dve):
                V = nc.vector
                for k in range(2):
                    V.memset(xT[k][D:D + 1, :], 1.0).then_inc(s_set, 1)
                V.memset(neg[:, 0, 0:1], 0.0).then_inc(s_g, 2)
                dve.wait_ge(s_g, 2)
                with dve.Fori(0, B // 2) as i:
                    own = Links(dve, s_own, 2 * LINKS * i)

                    def gate(k, t):
                        half, s = divmod(t, NB)
                        dve.wait_ge(s_s, 2 * NT * i + NT * k + t + 1)
                        V.tensor_tensor(gated[:, t % 2, :], m.bank[t % 2][:],
                                        m.gT[:, s, half * HALF:(half + 1) * HALF], ALU.mult).then_inc(s_g, 1)

                    def prelu(k):
                        dve.wait_ge(s_y, 2 * i + k + 1)
                        dve.wait_ge(s_hk, 32 * (2 * i + k) + 1)
                        y = m.bank[7][:].rearrange("p (c d) -> p c d", d=D)
                        own.link(V.tensor_scalar(neg[:], y, 0.0, m.a_col[:, 0:1], ALU.min, ALU.mult))
                        V.scalar_tensor_tensor(ln.h[:], y, 0.0, neg[:], ALU.max, ALU.add).then_inc(s_h, 1)
                        dve.wait_ge(s_h, 2 * i + k + 1)

                    def norm(k):
                        dve.wait_ge(s_sd, 2 * i + k + 1)
                        layernorm_norm(V, own, ln, s_n)

                    for t in range(NT):
                        gate(0, t)
                    for t in range(NT):
                        gate(1, t)
                        if t == 3:
                            prelu(0)
                        if t == 5:
                            layernorm_stats(V, own, ln, s_var)
                        if t == 8:
                            norm(0)
                    prelu(1)
                    layernorm_stats(V, own, ln, s_var)
                    norm(1)
                    assert own.n == 2 * LINKS, own.n


class Chain:

    def __init__(self, sb, sem, d, name):
        self.d = d
        self.tanh = sb(f"tanh_gates_{name}", [P, 4, B], F32)
        self.cell, self.forgot, self.added, self.out_gate, self.tanh_cell, self.h = (
            sb(f"{part}_{name}", [P, B], F32) for part in ("cell", "forgot", "added", "out_gate", "tanh_cell", "h"))
        (self.s_z_fg, self.s_z_io, self.s_t_fg, self.s_t_io, self.s_added, self.s_cell, self.s_tanh_cell,
         self.s_hi, self.s_h, self.s_lo) = (sem(f"{s}_{name}") for s in (
             "z_fg", "z_io", "t_fg", "t_io", "added", "cell", "tanh_cell", "hi", "h", "lo"))



def pe_gates(nc, pe, m, c, n, h_hi, h_lo, fg, io):
    z = (fg[:, 0, :], fg[:, 1, :], io[:, 0, :], io[:, 1, :])
    pe.wait_ge(c.s_hi, n + 1)
    for w in (m.u_lo[c.d], m.u_hi[c.d]):
        for g in range(4):
            nc.tensor.matmul(z[g], w[:, g, :], h_hi, start=False, stop=False, skip_group_check=True)
    pe.wait_ge(c.s_lo, n + 1)
    for g in range(4):
        last = nc.tensor.matmul(z[g], m.u_hi[c.d][:, g, :], h_lo, start=False, stop=True, skip_group_check=True)
        if g == G_:
            last.then_inc(c.s_z_fg, 1)
    last.then_inc(c.s_z_io, 1)


def act_gates(nc, act, c, n, fg, io):
    act.wait_ge(c.s_z_fg, n + 1)
    nc.scalar.activation(c.tanh[:, 0:2, :], fg, ACT.Tanh, scale=1.0 / Z_SCALE).then_inc(c.s_t_fg, 1)
    act.wait_ge(c.s_z_io, n + 1)
    nc.scalar.activation(c.tanh[:, 2:4, :], io, ACT.Tanh, scale=1.0 / Z_SCALE).then_inc(c.s_t_io, 1)


def act_cell(nc, act, c, n):
    act.wait_ge(c.s_cell, n + 1)
    nc.scalar.activation(c.tanh_cell[:], c.cell[:], ACT.Tanh, scale=0.5).then_inc(c.s_tanh_cell, 1)


def dve_terms(nc, dve, c, n):
    stt = nc.vector.scalar_tensor_tensor
    dve.wait_ge(c.s_t_fg, n + 1)
    stt(c.forgot[:], c.tanh[:, F_, :], 1.0, c.cell[:], ALU.add, ALU.mult)
    dve.wait_ge(c.s_t_io, n + 1)
    stt(c.added[:], c.tanh[:, I_, :], 1.0, c.tanh[:, G_, :], ALU.add, ALU.mult).then_inc(c.s_added, 1)


def dve_cell(nc, dve, c, n):
    nc.vector.tensor_scalar(c.out_gate[:], c.tanh[:, O_, :], 1.0, 0.5 * X_SCALE, ALU.add, ALU.mult)
    dve.wait_ge(c.s_added, n + 1)
    nc.vector.scalar_tensor_tensor(c.cell[:], c.forgot[:], 0.5, c.added[:], ALU.mult, ALU.add).then_inc(c.s_cell, 1)


def dve_hidden(nc, dve, c, n, h_hi):
    tt = nc.vector.tensor_tensor
    dve.wait_ge(c.s_tanh_cell, n + 1)
    tt(h_hi, c.out_gate[:], c.tanh_cell[:], ALU.mult).then_inc(c.s_hi, 1)
    tt(c.h[:], c.out_gate[:], c.tanh_cell[:], ALU.mult).then_inc(c.s_h, 1)


def dve_hidden_low(nc, dve, c, n, h_hi, h_lo):
    dve.wait_ge(c.s_h, n + 1)
    nc.vector.tensor_tensor(h_lo, c.h[:], h_hi, ALU.subtract).then_inc(c.s_lo, 1)


def encoder(nc, m):
    ctx, sb, sem = tools(nc)
    with ctx:
        ch = [Chain(sb, sem, d, name) for d, name in enumerate(("fwd", "bwd"))]
        s_set = sem("encoder_state_set")
        hello = sb("encoder_hello", [P, 1], F32)
        h = list(zip(m.enc_hi, m.enc_lo))

        banks = [[[m.bank[4 * d + 2 * p + j][:].rearrange("p (g t b) -> p g t b", g=2, t=CH) for j in range(2)]
                  for p in range(2)] for d in range(2)]

        def at(d, step):
            p, s = divmod(step, CH)
            s = CH - 1 - s if d else s
            return [z[:, :, s, :] for z in banks[d][p]]

        with nc.Block() as block:
            @block.tensor
            def _(pe):
                def fill(d, p, unit, col):
                    g, half = divmod(unit, 2)
                    z = banks[d][p][g // 2][:, g % 2, half * CH // 2:(half + 1) * CH // 2, :]
                    nc.tensor.matmul(z, m.w_hi[d][:, g, :], m.xs[:, bass.ds(col, HALFCH)],
                                     start=(unit % 4 == 0), stop=False, skip_group_check=True)
                    nc.tensor.matmul(z, m.w_lo[d][:, g, :], m.xs[:, bass.ds(col, HALFCH)],
                                     start=False, stop=False, skip_group_check=True)
                    nc.tensor.matmul(z, m.lstm_bias[d][:, g, :], m.ones3[:],
                                     start=False, stop=False, skip_group_check=True)

                for d in range(2):
                    for unit in range(8):
                        fill(d, 0, unit, COLS + (NCH - 1) * COLS * d + (unit % 2) * HALFCH)
                with pe.Fori(0, NCH // 2) as i:
                    for step in range(2 * CH):
                        p, s = divmod(step, CH)
                        for d in range(2):
                            fg, io = at(d, step)
                            pe_gates(nc, pe, m, ch[d], 2 * CH * i + step, h[d][0][:], h[d][1][:], fg, io)
                            if s % 2 == d:
                                unit = s // 2
                                col = (unit % 2) * HALFCH + (COLS * (NCH - 1 - p) - 2 * COLS * i if d else
                                                            COLS * (2 + p) + 2 * COLS * i)
                                fill(d, 1 - p, unit, col)

            @block.scalar
            def _(act):
                nc.scalar.activation(hello[:], m.ident[:, 0:1], ACT.Gelu)
                with act.Fori(0, NCH // 2) as i:
                    for step in range(2 * CH):
                        n = 2 * CH * i + step
                        act_cell(nc, act, ch[1], n)
                        act_gates(nc, act, ch[0], n, *at(0, step))
                        act_cell(nc, act, ch[0], n)
                        act_gates(nc, act, ch[1], n, *at(1, step))
                act_cell(nc, act, ch[1], T)

            @block.vector
            def _(dve):
                own = Links(dve, s_set)
                for d in range(2):
                    own.link(nc.vector.memset(ch[d].cell[:], 0.0))
                    own.link(nc.vector.memset(ch[d].out_gate[:], 0.0))
                nc.vector.memset(h[0][0][:], 0.0).then_inc(ch[0].s_hi, 1)
                nc.vector.memset(h[0][1][:], 0.0).then_inc(ch[0].s_lo, 1)
                nc.vector.memset(ch[1].cell[:], 0.0).then_inc(ch[1].s_cell, 1)
                with dve.Fori(0, NCH // 2) as i:
                    for step in range(2 * CH):
                        n = 2 * CH * i + step
                        for d in range(2):
                            late = 1 - d
                            dve_hidden(nc, dve, ch[late], n, h[late][0][:])
                            dve_terms(nc, dve, ch[d], n)
                            dve_hidden_low(nc, dve, ch[late], n, h[late][0][:], h[late][1][:])
                            dve_cell(nc, dve, ch[d], n)
                dve_hidden(nc, dve, ch[1], T, h[1][0][:])
                dve_hidden_low(nc, dve, ch[1], T, h[1][0][:], h[1][1][:])


BODY = 32
QS = BODY * B // P
LANES = P // B
RSQRT_SEED = 0x5f3759df


class Own:

    def __init__(self, dve, sem, base):
        self.dve, self.sem, self.base, self.n = dve, sem, base, 0

    def made(self, instruction):
        instruction.then_inc(self.sem, 1)
        self.n += 1

    def wait(self):
        self.dve.wait_ge(self.sem, self.base + self.n)


def decoder_and_experts(nc, m):
    ctx, sb, sem = tools(nc)
    with ctx:
        c = Chain(sb, sem, 2, "dec")
        ring_hi = sb("ring_hi", [P, QS, B, LANES], F16)
        ring_lo = sb("ring_lo", [P, QS, B, LANES], F16)
        h_at = lambda ring, step: ring[:, step % QS, :, step % BODY // QS]
        given = sb("given", [P, 4 * B], F32)
        left = sb("given_left", [P, 2, 4 * B], F32)
        parts = sb("given_parts", [P, 3, 4, B], BF16)
        s_given, s_parts, s_set = (sem(n) for n in ("given_made", "given_split", "decoder_set"))
        banks = [[m.bank[2 * p + j][:].rearrange("p (g t b) -> p g t b", g=2, t=CH) for j in range(2)]
                 for p in range(2)]

        wide = lambda name: sb(name, [P, QS, D], F32)
        one = lambda name: sb(name, [P, QS], F32)
        each = lambda name: sb("route_" + name, [P, QS, E], F32)
        res, h, h_kept, centred, square, normed, sums = (wide(n) for n in (
            "res", "ff_h", "ff_h_kept", "centred", "square", "normed", "sums"))
        split = sb("split", [P, QS, 2 * D], F16)
        total, mean, squares, var, half_bits, seed = (one(n) for n in (
            "total", "mean", "squares", "var", "half_bits", "rsqrt0"))
        newton = [[one(f"newton{k}_{part}") for part in ("square", "term", "rsqrt")] for k in range(3)]
        rank = sb("rank", [P, E], F32)
        rank_int = sb("rank_int", [P, E], mybir.dt.int32)
        score, equal0, ranked0, first, others, equal1, ranked1, second, chosen = (each(n) for n in (
            "score", "equal0", "ranked0", "first", "others", "equal1", "ranked1", "second", "chosen"))
        best = [one(f"best{k}") for k in range(4)]
        mask = sb("mask", [P, QS, 2 * E], BF16)
        xn = sb("xn", [P, HALF], F16)
        maskT = sb("maskT", [2 * E, HALF], BF16)
        hid = sb("hid", [HE, 2, HALF], F32)
        yT = sb("ff_yT", [D, HALF], F32)
        s_own = sem("ff_dve_step")
        (s_res, s_proj, s_h, s_hk, s_split, s_nT, s_xn, s_score, s_mask, s_mT, s_mk, s_pre, s_hid,
         s_ff, s_yT, s_yt, s_sum, s_out, s_rank) = (sem(n) for n in (
             "res_loaded", "projected", "ff_h_made", "ff_h_kept", "normed_split", "normed_turned",
             "xn_kept", "gate_scores", "mask_made", "mask_turned", "maskT_kept", "pre_made", "hid_made",
             "expert_done", "yT_kept", "y_turned", "sum_made", "sum_stored", "rank_made"))

        def tile_rows(tensor, j):
            return tensor.rearrange("b (j u c) d -> j b u (c d)", u=LANES, c=QS)[bass.ds(j, 1)]

        def past_first(j):
            return not (isinstance(j, int) and j == 0)

        flat = lambda z: z[:].rearrange("p c d -> p (c d)")
        NJ = T // BODY
        DVE_OWN = 33
        small = m.bank[4]
        y_bank = m.bank[7]
        pre_bank = [m.bank[5], m.bank[6]]
        over_d = lambda col: col[:].unsqueeze(2).broadcast_to([P, QS, D])
        over_e = lambda col: col[:].unsqueeze(2).broadcast_to([P, QS, E])

        def at(step):
            p, s = divmod(step, CH)
            return [z[:, :, s, :] for z in banks[p]]

        def bodies(engine, body):
            body(0, [])
            body(1, [(0, 0)])
            with engine.Fori(0, NJ - 2) as i:
                body(i + 2, [(i, BODY), (i + 1, 0)])

        def after(part):
            for s in range(2 * BODY):
                if s < BODY:
                    part(NJ - 2, s + BODY)
                part(NJ - 1, s)

        with nc.Block() as block:
            @block.sync
            def _(sp):
                def load(j):
                    sp.dma_start(flat(res), tile_rows(m.kept, j)).then_inc(s_res, 16)

                def store(j):
                    sp.wait_ge(s_sum, j + 1)
                    sp.dma_start(tile_rows(m.out, j), flat(sums)).then_inc(s_out, 16)

                load(0)
                sp.wait_ge(s_h, 1)
                load(1)
                with sp.Fori(0, NJ - 2) as i:
                    sp.wait_ge(s_h, i + 2)
                    load(i + 2)
                    store(i)
                store(NJ - 2)
                store(NJ - 1)
                sp.wait_ge(s_out, 16 * NJ + 1)

            @block.gpsimd
            def _(pool):
                G = nc.gpsimd
                G.iota(rank_int[:], pattern=[[-1, E]], base=E, channel_multiplier=0).then_inc(s_rank, 1)
                pool.wait_ge(s_rank, 1)
                G.tensor_copy(rank[:], rank_int[:]).then_inc(s_rank, 1)

            @block.tensor
            def _(pe):
                mm = nc.tensor.matmul

                def fill(p, unit):
                    g, half = divmod(unit, 2)
                    z = banks[p][g // 2][:, g % 2, half * CH // 2:(half + 1) * CH // 2, :]
                    for k in range(3):
                        mm(z, m.identb[:], parts[:, k, g, :].unsqueeze(1).broadcast_to([P, CH // 2, B]),
                           start=(unit % 4 == 0 and k == 0), stop=False, skip_group_check=True)

                def pre_x(j, e):
                    if e < 2:
                        if e == 0 and past_first(j):
                            pe.wait_ge(s_sum, j)
                    else:
                        pe.wait_ge(s_hid, E * j + e - 1)
                    mm(pre_bank[e % 2][:], m.w1_hi[:, e, :], xn[:], start=True, stop=False)
                    mm(pre_bank[e % 2][:], m.w1_lo[:, e, :], xn[:], start=False, stop=False)

                def pre_mask(j, e):
                    mm(pre_bank[e % 2][:], m.pick[:, e, :], maskT[:], start=False, stop=True).then_inc(s_pre, 1)

                def pe_part(j, s):
                    if s == 0:
                        pe.wait_ge(c.s_lo, BODY * (j + 1) + 1)
                        for blk in range(QS):
                            z = small[:, blk * D:(blk + 1) * D]
                            mm(z, m.ones3[:], m.wo_bias, start=(blk == 0), stop=False, skip_group_check=True)
                            for ring, wo in ((ring_hi, m.wo_hi), (ring_hi, m.wo_lo), (ring_lo, m.wo_hi)):
                                last = mm(z, ring[:, blk].rearrange("p b u -> p (b u)"), wo[:], start=False, stop=True, skip_group_check=True)
                        last.then_inc(s_proj, 1)
                    if s == 7:
                        pe.wait_ge(s_split, j + 1)
                        for blk in range(QS):
                            last = nc.tensor.transpose(
                                small[:, HALF // 2:].bitcast(F16)[:, blk * P:(blk + 1) * P], split[:, blk, :],
                                m.ident16[:])
                        last.then_inc(s_nT, 1)
                    if s == 8:
                        pe.wait_ge(s_xn, j + 1)
                        for blk in range(QS):
                            x, z = xn[:, blk * P:(blk + 1) * P], small[:, blk * E:(blk + 1) * E]
                            mm(z, m.ones3[:], m.gate_bias, start=(blk == 0), stop=False, skip_group_check=True)
                            mm(z, x, m.wg_hi[:], start=False, stop=False, skip_group_check=True)
                            last = mm(z, x, m.wg_lo[:], start=False, stop=True, skip_group_check=True)
                        last.then_inc(s_score, 1)
                    if s in (10, 11):
                        pre_x(j, s - 10)
                    if s == 13:
                        pe.wait_ge(s_mask, j + 1)
                        for blk in range(QS):
                            last = nc.tensor.transpose(
                                small[:, HALF // 2:].bitcast(BF16)[0:2 * E, blk * P:(blk + 1) * P], mask[:, blk, :],
                                m.identb[:])
                        last.then_inc(s_mT, 1)
                    if s == 14:
                        pe.wait_ge(s_mk, j + 1)
                        pre_mask(j, 0)
                        pre_mask(j, 1)
                    if s == 15:
                        for part in range(3):
                            mm(y_bank[0:D, :], m.b2[:, part, :], maskT[:], start=(part == 0), stop=False)
                    if 16 <= s < 16 + 2 * E:
                        e, odd = divmod(s - 16, 2)
                        if not odd:
                            pe.wait_ge(s_hid, E * j + e + 1)
                            mm(y_bank[0:D, :], m.w2[:, e, :], hid[:, e % 2, :], start=False, stop=(e == E - 1)
                               ).then_inc(s_ff, 1)
                        elif e + 2 < E:
                            pre_x(j, e + 2)
                            pre_mask(j, e + 2)
                    if s in (32, 33):
                        if s == 32:
                            pe.wait_ge(s_yT, j + 1)
                        for blk in range(2 * (s - 32), 2 * (s - 32) + 2):
                            last = mm(pre_bank[0][:, blk * D:(blk + 1) * D], yT[:, blk * P:(blk + 1) * P],
                                      m.ident[0:D, 0:D], start=(blk == 0), stop=True, skip_group_check=True)
                        if s == 33:
                            last.then_inc(s_yt, 1)

                z = m.bank[4][:, 0:4 * B]
                for g in range(4):
                    zg = z[:, g * B:(g + 1) * B]
                    first_of_bank = g == 0
                    for d in range(2):
                        for w, v in ((m.wd_hi, m.enc_hi), (m.wd_lo, m.enc_hi), (m.wd_hi, m.enc_lo)):
                            mm(zg, w[d][:, g, :], v[d][:], start=first_of_bank, stop=False, skip_group_check=True)
                            first_of_bank = False
                    last = mm(zg, m.lstm_bias[2][:, g, :], m.ones3[:, 0:B], start=False, stop=True,
                              skip_group_check=True)
                last.then_inc(s_given, 1)
                pe.wait_ge(s_parts, 1)
                for unit in range(8):
                    fill(0, unit)

                def body(i, tiles):
                    for step in range(BODY):
                        p, s = divmod(step, CH)
                        before = (step - 1) % BODY
                        pe_gates(nc, pe, m, c, BODY * i + step, h_at(ring_hi, before), h_at(ring_lo, before), *at(step))
                        if s % 2:
                            fill(1 - p, s // 2)
                        for j, start in tiles:
                            pe_part(j, start + step)

                bodies(pe, body)
                after(pe_part)

            @block.scalar
            def _(act):
                S = nc.scalar

                def act_part(j, s):
                    if s == 5:
                        act.wait_ge(s_h, j + 1)
                        if past_first(j):
                            act.wait_ge(s_sum, j)
                        S.copy(h_kept[:], h[:]).then_inc(s_hk, 1)
                    if s == 7:
                        act.wait_ge(s_nT, j + 1)
                        S.copy(xn[:], small[:, HALF // 2:].bitcast(F16)).then_inc(s_xn, 1)
                    if s == 13:
                        act.wait_ge(s_mT, j + 1)
                        S.copy(maskT[:], small[:, HALF // 2:].bitcast(BF16)[0:2 * E, :]).then_inc(s_mk, 1)
                    if s in (14,) + tuple(range(16, 16 + 2 * (E - 1), 2)):
                        e = 0 if s == 14 else (s - 14) // 2
                        act.wait_ge(s_pre, E * j + e + 1)
                        S.activation(hid[:, e % 2, :], pre_bank[e % 2][:], ACT.Gelu, scale=1.0 / Z_SCALE,
                                     bias=m.b1[:, e:e + 1]).then_inc(s_hid, 1)
                    if s == 31:
                        act.wait_ge(s_ff, E * (j + 1))
                        S.copy(yT[:], y_bank[0:D, :]).then_inc(s_yT, 1)

                def body(i, tiles):
                    for step in range(BODY):
                        n = BODY * i + step
                        act_gates(nc, act, c, n, *at(step))
                        act_cell(nc, act, c, n)
                        for j, start in tiles:
                            act_part(j, start + step)

                bodies(act, body)
                after(act_part)

            @block.vector
            def _(dve):
                V = nc.vector
                own = Links(dve, s_set)
                own.link(V.memset(c.cell[:], 0.0))
                V.memset(sums[:], 0.0).then_inc(s_out, 1)
                V.memset(h_at(ring_hi, BODY - 1), 0.0).then_inc(c.s_hi, 1)
                V.memset(h_at(ring_lo, BODY - 1), 0.0).then_inc(c.s_lo, 1)
                dve.wait_ge(s_given, 1)
                own.link(V.tensor_copy(given[:], m.bank[4][:, 0:4 * B]))
                third = parts[:].rearrange("p k g b -> p k (g b)")
                own.link(V.tensor_copy(third[:, 0], given[:]))
                own.link(V.tensor_tensor(left[:, 0], given[:], third[:, 0], ALU.subtract))
                own.link(V.tensor_copy(third[:, 1], left[:, 0]))
                own.link(V.tensor_tensor(left[:, 1], left[:, 0], third[:, 1], ALU.subtract))
                V.tensor_copy(third[:, 2], left[:, 1]).then_inc(s_parts, 1)
                dve.wait_ge(s_rank, 2)

                TT, TS, STT, RED = V.tensor_tensor, V.tensor_scalar, V.scalar_tensor_tensor, V.tensor_reduce
                ranks = rank[:].unsqueeze(1).broadcast_to([P, QS, E])
                INT = mybir.dt.int32

                def in_gates(j, s, own):
                    do = own.made
                    if s == 0:
                        dve.wait_ge(s_proj, j + 1)
                        dve.wait_ge(s_res, 16 * j + 16)
                        if past_first(j):
                            dve.wait_ge(s_hk, j)
                        STT(flat(h), small[:, 0:QS * D], 1.0 / Z_SCALE, flat(res), ALU.mult, ALU.add).then_inc(s_h, 1)
                    if s == 1:
                        own.wait()
                        do(TS(mean[:], total[:], 1.0 / D, None, ALU.mult))
                        own.wait()
                        do(TT(centred[:], h[:], over_d(mean), ALU.subtract))
                    if s == 2:
                        own.wait()
                        do(RED(squares[:], square[:], AX.X, ALU.add))
                        own.wait()
                        do(TS(var[:], squares[:], 1.0 / D, EPS, ALU.mult, ALU.add))
                    if s == 3:
                        own.wait()
                        do(TS(seed[:].bitcast(INT), half_bits[:].bitcast(INT), -1.0, float(RSQRT_SEED), ALU.mult, ALU.add))
                        newton_square(own, 0)
                        newton_term(own, 0)
                    if s == 4:
                        newton_square(own, 1)
                        newton_term(own, 1)
                        newton_last(own, 1)
                    if s == 5:
                        newton_term(own, 2)
                        newton_last(own, 2)
                    if s == 6:
                        own.wait()
                        do(TS(split[:, :, 0:D], normed[:], X_SCALE, None, ALU.mult))
                        own.wait()
                        STT(split[:, :, D:2 * D], normed[:], X_SCALE, split[:, :, 0:D], ALU.mult, ALU.subtract
                            ).then_inc(s_split, 1)
                    if s == 8:
                        dve.wait_ge(s_score, j + 1)
                        do(V.tensor_copy(score[:], small[:, 0:QS * E].rearrange("p (q e) -> p q e", e=E)))
                        own.wait()
                        do(RED(best[0][:], score[:], AX.X, ALU.max))
                        own.wait()
                        do(TT(equal0[:], score[:], over_e(best[0]), ALU.is_equal))
                    if s == 9:
                        own.wait()
                        do(RED(best[1][:], ranked0[:], AX.X, ALU.max))
                        own.wait()
                        do(TT(first[:], ranked0[:], over_e(best[1]), ALU.is_equal))
                        own.wait()
                        do(STT(others[:], first[:], -3e38, score[:], ALU.mult, ALU.add))
                    if s == 10:
                        own.wait()
                        do(TT(equal1[:], others[:], over_e(best[2]), ALU.is_equal))
                        own.wait()
                        do(TT(ranked1[:], equal1[:], ranks, ALU.mult))
                        own.wait()
                        do(RED(best[3][:], ranked1[:], AX.X, ALU.max))
                    if s == 11:
                        own.wait()
                        do(TT(chosen[:], first[:], second[:], ALU.add))
                        own.wait()
                        do(TS(mask[:, :, 0:E], chosen[:], -1.0, None, ALU.add))
                        V.tensor_copy(mask[:, :, E:2 * E], chosen[:]).then_inc(s_mask, 1)
                        assert own.n == DVE_OWN, own.n
                    if s == 34:
                        dve.wait_ge(s_yt, j + 1)
                        dve.wait_ge(s_hk, j + 1)
                        dve.wait_ge(s_out, 16 * j + 1)
                        TT(flat(sums), pre_bank[0][:, 0:QS * D], flat(h_kept), ALU.add).then_inc(s_sum, 1)

                def newton_square(own, k):
                    own.wait()
                    r = newton[k - 1][2] if k else seed
                    own.made(TT(newton[k][0][:], r[:], r[:], ALU.mult))

                def newton_term(own, k):
                    own.wait()
                    own.made(STT(newton[k][1][:], newton[k][0][:], -0.5, var[:], ALU.mult, ALU.mult))

                def newton_last(own, k):
                    own.wait()
                    r = newton[k - 1][2] if k else seed
                    own.made(STT(newton[k][2][:], newton[k][1][:], 1.5, r[:], ALU.add, ALU.mult))

                def in_tanh(j, s, own):
                    do = own.made
                    if s == 1:
                        dve.wait_ge(s_h, j + 1)
                        do(RED(total[:], h[:], AX.X, ALU.add))
                    if s == 2:
                        own.wait()
                        do(TT(square[:], centred[:], centred[:], ALU.mult))
                    if s == 3:
                        own.wait()
                        do(TS(half_bits[:].bitcast(INT), var[:].bitcast(INT), 1, None, ALU.logical_shift_right))
                    if s == 4:
                        newton_last(own, 0)
                    if s == 5:
                        newton_square(own, 2)
                    if s == 6:
                        own.wait()
                        do(TT(normed[:], centred[:], over_d(newton[2][2]), ALU.mult))
                    if s == 9:
                        own.wait()
                        do(TT(ranked0[:], equal0[:], ranks, ALU.mult))
                    if s == 10:
                        own.wait()
                        do(RED(best[2][:], others[:], AX.X, ALU.max))
                    if s == 11:
                        own.wait()
                        do(TT(second[:], ranked1[:], over_e(best[3]), ALU.is_equal))

                def part(window, tiles, step):
                    for j, start, own in tiles:
                        window(j, start + step, own)

                def body(i, tiles):
                    tiles = [(j, start, Own(dve, s_own, DVE_OWN * j)) for j, start in tiles]
                    for step in range(BODY):
                        n = BODY * i + step
                        dve_terms(nc, dve, c, n)
                        dve_cell(nc, dve, c, n)
                        part(in_tanh, tiles, step)
                        if step == 0 and tiles:
                            dve.wait_ge(s_proj, tiles[-1][0] + 1)
                        dve_hidden(nc, dve, c, n, h_at(ring_hi, step))
                        dve_hidden_low(nc, dve, c, n, h_at(ring_hi, step), h_at(ring_lo, step))
                        part(in_gates, tiles, step)

                bodies(dve, body)
                owns = {}

                def last_part(j, s):
                    if s in (0, BODY):
                        owns[j] = Own(dve, s_own, DVE_OWN * j)
                    in_tanh(j, s, owns[j])
                    in_gates(j, s, owns[j])
                after(last_part)


def kernel(**inputs):
    import numpy as _np
    import concourse.bacc as _bacc
    from concourse import mybir as _mybir
    from concourse.bass_utils import run_bass_kernel_spmd as _run

    nc = _bacc.Bacc("TRN2", target_bir_lowering=False, num_devices=1)
    arrays, args = {}, {}
    for name in sorted(inputs):
        array = _np.ascontiguousarray(inputs[name])
        arrays[f"in_{name}_dram"] = array
        args[name] = nc.dram_tensor(f"in_{name}_dram", array.shape, _mybir.dt.from_np(array.dtype),
                                    kind="ExternalInput").ap()
    out = nc.dram_tensor("out_dram", (B, T, D), _mybir.dt.float32, kind="ExternalOutput").ap()
    build(nc, args, out)
    r = _run(nc, [arrays], core_ids=[0])
    return r.results[0]["out_dram"]
```

```python
from contextlib import ExitStack

import numpy as np
import concourse.bass as bass
from concourse import mybir

F32, F16, BF16 = mybir.dt.float32, mybir.dt.float16, mybir.dt.bfloat16
ALU = mybir.AluOpType
ACT = mybir.ActivationFunctionType
AX = mybir.AxisListType

P = 128
B, T, D = 16, 1024, 64
H = 128
E, HE = 8, 128
NB = T // P
HALF = 512
EPS = 1e-5

W_SCALE = 2.0 ** 6
X_SCALE = 2.0 ** 12
Z_SCALE = W_SCALE * X_SCALE
MIX_SCALE = 2.0 ** 6
F_, I_, G_, O_ = range(4)
GATE_FROM = (1, 0, 2, 3)
GATE_SCALE = (0.5 * W_SCALE, 0.5 * W_SCALE, W_SCALE, 0.5 * W_SCALE)

CH = 16
COLS = CH * B
NCH = T // CH
HALFCH = COLS // 2
BIAS_MIX = 12 * H + D + E
NBIAS = BIAS_MIX + 5 * D
BIG = 2.0 ** 100


def tools(nc):
    ctx = ExitStack()
    return (ctx, lambda name, shape, dt: ctx.enter_context(nc.sbuf_tensor(name, shape, dt)),
            lambda name: ctx.enter_context(nc.semaphore(name)))


class Links:

    def __init__(self, engine, sem, base=0):
        self.engine, self.sem, self.base, self.n = engine, sem, base, 0

    def link(self, instruction):
        instruction.then_inc(self.sem, 1)
        self.n += 1
        self.engine.wait_ge(self.sem, self.base + self.n)


class Own:

    def __init__(self, dve, sem, base):
        self.dve, self.sem, self.base, self.n = dve, sem, base, 0

    def made(self, instruction):
        instruction.then_inc(self.sem, 1)
        self.n += 1

    def wait(self):
        self.dve.wait_ge(self.sem, self.base + self.n)


class Shared:
    pass


def build(nc, a, out):
    ctx = ExitStack()
    m = Shared()
    m.a, m.out = a, out

    def sb(name, shape, dt):
        return ctx.enter_context(nc.sbuf_tensor(name, shape, dt))

    with ctx:
        m.bank = [ctx.enter_context(nc.psum_tensor(f"bank{k}", [P, HALF], F32)) for k in range(8)]
        m.ident = sb("ident", [P, P], F32)
        m.ident16 = sb("ident16", [P, P], F16)
        m.identb = sb("identb", [P, P], BF16)
        m.kept = nc.dram_tensor("kept_h", (B, T, D), F32, kind="Internal").ap()
        m.gT = sb("gammaT", [P, NB, T], F32)
        m.xs = sb("xs", [P, T * B + 2 * COLS], F16)
        m.u_hi = [sb(f"u_hi{d}", [P, 4, H], F16) for d in range(3)]
        m.u_lo = [sb(f"u_lo{d}", [P, 4, H], F16) for d in range(3)]
        m.w_hi = [sb(f"w_hi{d}", [P, 4, H], F16) for d in range(2)]
        m.w_lo = [sb(f"w_lo{d}", [P, 4, H], F16) for d in range(2)]
        m.wd_hi = [sb(f"wd_hi{d}", [P, 4, H], F16) for d in range(2)]
        m.wd_lo = [sb(f"wd_lo{d}", [P, 4, H], F16) for d in range(2)]
        m.bias = sb("bias", [3, NBIAS], BF16)
        m.lstm_bias = [m.bias[:, 4 * H * d:4 * H * (d + 1)].rearrange("p (g h) -> p g h", g=4)
                       for d in range(3)]
        m.wo_bias = m.bias[:, 12 * H:12 * H + D]
        m.gate_bias = m.bias[:, 12 * H + D:12 * H + D + E]
        m.q_bias, m.k_bias = (m.bias[:, BIAS_MIX + k * 2 * D:BIAS_MIX + (k + 1) * 2 * D] for k in range(2))
        m.vo_bias = m.bias[:, BIAS_MIX + 4 * D:]
        m.ones3 = sb("ones3", [3, P], BF16)
        m.ones_s = sb("ones_s", [3, HALF], BF16)
        m.a_col = sb("a_col", [P, 1], F32)
        m.bo_col = sb("bo_col", [P, 1], F32)
        m.wo_hi = sb("wo_hi", [P, D], F16)
        m.wo_lo = sb("wo_lo", [P, D], F16)
        m.wg_hi = sb("wg_hi", [P, E], F16)
        m.wg_lo = sb("wg_lo", [P, E], F16)
        m.w1_hi = sb("w1_hi", [P, E, HE], F16)
        m.w1_lo = sb("w1_lo", [P, E, HE], F16)
        m.w2 = sb("w2", [HE, E, D], F32)
        m.b1 = sb("b1", [HE, E], F32)
        m.b2 = sb("b2", [2 * E, 3, D], BF16)
        m.pick = sb("pick", [2 * E, E, HE], BF16)
        m.wq_hi, m.wq_lo, m.wk_hi, m.wk_lo = (sb(n, [P, 2, D], F16) for n in ("wq_hi", "wq_lo", "wk_hi", "wk_lo"))
        m.wvo_hi, m.wvo_lo = (sb(n, [P, D], F16) for n in ("wvo_hi", "wvo_lo"))
        m.enc_hi = [sb(f"enc_hi{d}", [P, B], F16) for d in range(2)]
        m.enc_lo = [sb(f"enc_lo{d}", [P, B], F16) for d in range(2)]

        raw_ctx, raw_sb, raw_sem = tools(nc)
        with raw_ctx:
            m.raw_u = [raw_sb(f"raw_u{d}", [P, 4 * H], F32) for d in range(3)]
            m.raw_w = [raw_sb(f"raw_w{d}", [P, 4 * H], F32) for d in range(2)]
            m.raw_wd = [raw_sb(f"raw_wd{d}", [P, 4 * H], F32) for d in range(2)]
            m.raw_wo = raw_sb("raw_wo", [P, D], F32)
            m.raw_wg = raw_sb("raw_wg", [P, E], F32)
            m.raw_w1 = raw_sb("raw_experts", [P, E, HE], F32)
            m.raw_b = raw_sb("raw_b", [3, BIAS_MIX], F32)
            m.raw_b2 = raw_sb("raw_b2", [2 * E, 3, D], F32)
            m.s_raw = raw_sem("raw_loaded")
            setup(nc, m)
            token_mixing(nc, m)
        encoder(nc, m)
        decoder_and_experts(nc, m)


def setup(nc, m):
    a = m.a
    ctx, sb, sem = tools(nc)
    with ctx:
        raw_mix = sb("raw_mix", [3, 5 * D], F32)
        part = sb("part", [3, 3, 5 * D], BF16)
        left = sb("left", [3, 3, 5 * D], F32)
        raw_qk = [sb(f"raw_{n}", [P, D], F32) for n in "qk"]
        wv = sb("wv", [D, D], F32)
        bv = sb("bv", [D, 1], F32)
        tok_wo = sb("tok_wo", [D, D], F32)
        wvT = sb("wvT", [D, 2, D], F32)
        bv3 = sb("bv3", [D, 3], F32)
        raw_wvo = sb("raw_wvo", [P, D], F32)
        g_rows = [sb(f"g_rows{k}", [P, T], F32) for k in range(NB)]
        s_w, s_b, s_dve, s_z, s_id, s_id0 = (sem(n) for n in
            ("weights_loaded", "vectors_loaded", "split_step", "b2_zeroed", "ident_made", "ident_zeroed"))
        s_g = [sem(f"gamma_loaded{k}") for k in range(NB)]
        s_gt, s_gfree, s_v, s_vk = (sem(n) for n in
            ("gamma_turned", "gamma_banks_free", "wv_on_pe", "wv_kept"))
        n_w, n_b, n_raw = [0], [0], [0]

        with nc.Block() as block:
            @block.sync
            def _(sp):
                def load(dst, src, s=s_w, n=n_w, scattered=False):
                    sp.dma_start(dst, src, allow_slow_non_contiguous=scattered).then_inc(s, 16)
                    n[0] += 16

                for k in range(NB):
                    sp.dma_start(g_rows[k][:], a["L0_tok_d_gamma_batched"][k * P:(k + 1) * P, :]).then_inc(s_g[k], 16)
                load(wv[:], a["L0_tok_Wv"])
                load(bv[:], a["L0_tok_bv"][:, None])
                load(tok_wo[:], a["L0_tok_Wo"])
                for raw, w in zip(raw_qk, (a["L0_tok_Wq"], a["L0_tok_Wk"])):
                    for k in range(2):
                        load(raw[k * D:(k + 1) * D, :], w)
                for k in range(2):
                    load(m.bo_col[k * D:(k + 1) * D, :], a["L0_tok_bo"][:, None])
                load(m.a_col[:], a["L0_tok_prelu_a"][None, :].broadcast_to([P, 1]))
                for k, name in enumerate(("bq", "bq", "bk", "bk")):
                    load(raw_mix[:, k * D:(k + 1) * D], a["L0_tok_" + name][None, :].broadcast_to([3, D]), s_b, n_b)

                def load_raw(dst, src, scattered=False):
                    load(dst, src, m.s_raw, n_raw, scattered)

                for d, u in enumerate((a["L0_attn_Uf"], a["L0_attn_Ub"], a["L0_attn_Ud"])):
                    load_raw(m.raw_u[d][:], u)
                for d, w in enumerate((a["L0_attn_Wf"], a["L0_attn_Wb"])):
                    load_raw(m.raw_w[d][0:D, :], w)
                    load_raw(m.raw_w[d][D:2 * D, :], w)
                for d in range(2):
                    load_raw(m.raw_wd[d][:], a["L0_attn_Wd"][H * d:H * (d + 1), :])
                load_raw(m.raw_wo[:], a["L0_attn_Wo"])
                for k in range(2):
                    load_raw(m.raw_wg[k * D:(k + 1) * D, :], a["L0_ffn_Wg"])
                    load_raw(m.raw_w1[k * D:(k + 1) * D, :, :], a["L0_ffn_W1"].rearrange("e d h -> d e h"))
                load_raw(m.w2[:], a["L0_ffn_W2"].rearrange("e h d -> h e d"))
                load_raw(m.b1[:], a["L0_ffn_b1"].rearrange("e h -> h e"), scattered=True)
                at = 0
                for name in ("attn_bf", "attn_bb", "attn_bd", "attn_bo", "ffn_bg"):
                    b = a["L0_" + name]
                    load_raw(m.raw_b[:, at:at + b.shape[0]], b[None, :].broadcast_to([3, b.shape[0]]))
                    at += b.shape[0]
                sp.wait_ge(s_z, 1)
                load_raw(m.raw_b2[E:2 * E, 0, :], a["L0_ffn_b2"])
                m.n_raw = n_raw[0]

            @block.gpsimd
            def _(pool):
                nc.gpsimd.memset(m.ident[:], 0.0).then_inc(s_id0, 1)
                pool.wait_ge(s_id0, 1)
                nc.gpsimd.affine_select(out=m.ident[:], in_=m.ident[:], compare_op=ALU.not_equal, fill=1.0,
                                        base=0, pattern=[[-1, P]], channel_multiplier=1).then_inc(s_id, 1)
                nc.gpsimd.memset(m.raw_b2[:], 0.0).then_inc(s_z, 1)
                nc.gpsimd.memset(m.ones3[:], Z_SCALE)
                nc.gpsimd.memset(m.ones_s[:], MIX_SCALE ** 2)
                nc.gpsimd.memset(m.xs[:, 0:COLS], 0.0)
                nc.gpsimd.memset(m.xs[:, COLS + T * B:], 0.0)

            @block.tensor
            def _(pe):
                pe.wait_ge(s_id, 1)
                for k in range(NB):
                    pe.wait_ge(s_g[k], 16)
                    for half in range(2):
                        n = 2 * k + half
                        if n >= 4:
                            pe.wait_ge(s_gfree, n - 3)
                        for s in range(4):
                            blk = 4 * half + s
                            last = nc.tensor.transpose(m.bank[n % 4][:, s * P:(s + 1) * P],
                                                       g_rows[k][:, blk * P:(blk + 1) * P], m.ident[:])
                        last.then_inc(s_gt, 1)
                pe.wait_ge(s_w, n_w[0])
                nc.tensor.transpose(m.bank[4][0:D, 0:D], wv[:], m.ident[0:D, 0:D]).then_inc(s_v, 1)
                pe.wait_ge(s_vk, 1)
                nc.tensor.matmul(m.bank[5][:, 0:D], wvT[:].rearrange("p two d -> p (two d)"), tok_wo[:],
                                 start=True, stop=True).then_inc(s_v, 1)
                nc.tensor.matmul(m.bank[6][0:3, 0:D], bv3[:], tok_wo[:], start=True, stop=True).then_inc(s_v, 1)

            @block.scalar
            def _(act):
                for k in range(NB):
                    for half in range(2):
                        n = 2 * k + half
                        act.wait_ge(s_gt, n + 1)
                        nc.scalar.copy(m.gT[:, 4 * half:4 * half + 4, k * P:(k + 1) * P],
                                       m.bank[n % 4][:].rearrange("p (s t) -> p s t", s=4)).then_inc(s_gfree, 1)
                act.wait_ge(s_v, 1)
                nc.scalar.copy(bv3[:], bv[:].broadcast_to([D, 3]))
                nc.scalar.copy(wvT[:], m.bank[4][0:D, 0:D].unsqueeze(1).broadcast_to([D, 2, D])).then_inc(s_vk, 1)
                act.wait_ge(s_v, 2)
                nc.scalar.copy(raw_wvo[:], m.bank[5][:, 0:D]).then_inc(s_vk, 1)
                act.wait_ge(s_v, 3)
                nc.scalar.copy(raw_mix[:, 4 * D:], m.bank[6][0:3, 0:D]).then_inc(s_vk, 1)

            @block.vector
            def _(dve):
                own = Links(dve, s_dve)
                V = nc.vector
                dve.wait_ge(s_id, 1)
                V.tensor_copy(m.ident16[:], m.ident[:])
                V.tensor_copy(m.identb[:], m.ident[:])
                V.tensor_scalar(m.pick[:], m.ident[0:2 * E, 0:E].unsqueeze(2).broadcast_to([2 * E, E, HE]), BIG, None, ALU.mult)
                dve.wait_ge(s_w, n_w[0])

                for high, low, raw in ((m.wq_hi, m.wq_lo, raw_qk[0]), (m.wk_hi, m.wk_lo, raw_qk[1])):
                    split(V, own, high[:], low[:], raw[:].unsqueeze(1).broadcast_to([P, 2, D]), MIX_SCALE)
                dve.wait_ge(s_vk, 2)
                split(V, own, m.wvo_hi[:], m.wvo_lo[:], raw_wvo[:], MIX_SCALE)
                dve.wait_ge(s_b, n_b[0])
                dve.wait_ge(s_vk, 3)
                bias_rows(V, own, m, m.bias[:, BIAS_MIX:], raw_mix[:], part, left)


def split(engine, own, high, low, raw, scale):
    own.link(engine.tensor_scalar(high, raw, scale, None, ALU.mult))
    engine.scalar_tensor_tensor(low, raw, scale, high, ALU.mult, ALU.subtract)


def split_in_place(engine, own, high, low, raw, scale):
    own.link(engine.tensor_scalar(raw, raw, scale, None, ALU.mult))
    own.link(engine.tensor_copy(high, raw))
    engine.tensor_tensor(low, raw, high, ALU.subtract)


def thirds(engine, own, value, part, left):
    own.link(engine.tensor_copy(part[:, 0], value))
    own.link(engine.tensor_tensor(left[:, 0], value, part[:, 0], ALU.subtract))
    own.link(engine.tensor_copy(part[:, 1], left[:, 0]))
    own.link(engine.tensor_tensor(left[:, 1], left[:, 0], part[:, 1], ALU.subtract))
    own.link(engine.tensor_copy(part[:, 2], left[:, 1]))


def bias_rows(engine, own, m, rows, value, part, left):
    thirds(engine, own, value, part, left)
    own.link(engine.tensor_scalar(left[:, 0], part[:, 0], m.ident[0:3, 0:1], None, ALU.mult))
    own.link(engine.tensor_scalar(left[:, 1], part[:, 1], m.ident[0:3, 1:2], None, ALU.mult))
    own.link(engine.tensor_tensor(left[:, 2], left[:, 0], left[:, 1], ALU.add))
    own.link(engine.tensor_scalar(left[:, 1], part[:, 2], m.ident[0:3, 2:3], None, ALU.mult))
    own.link(engine.tensor_tensor(rows, left[:, 2], left[:, 1], ALU.add))


def split_weights(engine, own, m, part, left):
    lstm = ([(m.u_hi[d], m.u_lo[d], m.raw_u[d]) for d in range(3)]
            + [(m.w_hi[d], m.w_lo[d], m.raw_w[d]) for d in range(2)]
            + [(m.wd_hi[d], m.wd_lo[d], m.raw_wd[d]) for d in range(2)])
    for high, low, raw in lstm:
        for g in range(4):
            k = GATE_FROM[g] * H
            split_in_place(engine, own, high[:, g, :], low[:, g, :], raw[:, k:k + H], GATE_SCALE[g])
    split_in_place(engine, own, m.wo_hi[:], m.wo_lo[:], m.raw_wo[:], W_SCALE)
    split_in_place(engine, own, m.wg_hi[:], m.wg_lo[:], m.raw_wg[:], W_SCALE)
    split_in_place(engine, own, m.w1_hi[:], m.w1_lo[:], m.raw_w1[:], W_SCALE)
    for d in range(3):
        for g in (F_, I_, O_):
            k = (4 * d + GATE_FROM[g]) * H
            own.link(engine.tensor_scalar(m.raw_b[:, k:k + H], m.raw_b[:, k:k + H], 0.5, None, ALU.mult))
    bias_rows(engine, own, m, m.bias[:, 0:BIAS_MIX], m.raw_b[:], part, left)
    thirds(engine, own, m.raw_b2[:, 0, :], m.b2, m.raw_b2[:, 1:3, :])


TOKENS_OF = [4 * (q % 2) + q // 2 for q in range(NB)]


class Layernorm:

    def __init__(self, sb, name):
        one = lambda part: sb(name + part, [P, NB], F32)
        self.h, self.centred, self.square = (sb(name + part, [P, NB, D], F32) for part in ("h", "centred", "square"))
        self.split = sb(name + "split", [P, NB, 2 * D], F16)
        self.total, self.mean, self.squares, self.var, self.dev = (one(p) for p in
                                                                   ("total", "mean", "squares", "var", "dev"))
        self.r0, self.t1, self.t2, self.t3, self.r = (one(p) for p in ("r0", "t1", "t2", "t3", "r"))


def over_tokens(column):
    return column.unsqueeze(2).broadcast_to([P, NB, D])


def token_mixing(nc, m):
    a = m.a
    ctx, sb, sem = tools(nc)
    NT = 2 * NB
    RING = 3
    LINKS = 11
    with ctx:
        x_rows = [sb(f"x_rows{k}", [P, NB, D], F32) for k in range(2)]
        x_split = sb("x_split", [P, NB, 2 * D], F16)
        xT = sb("xT", [P, T], F16)
        q_hi = [sb(f"q_hi{k}", [P, T], F16) for k in range(2)]
        q_lo = [sb(f"q_lo{k}", [P, T], F16) for k in range(2)]
        k_both = [sb(f"k_both{k}", [P, T], F16) for k in range(2)]
        vo = [sb(f"vo{k}", [P, NB, D], F32) for k in range(2)]
        yT = sb("yT", [P, HALF], F32)
        gated = sb("gated", [P, RING, HALF], F32)
        neg = sb("neg", [P, NB, D], F32)
        hello = sb("hello", [P, 4], F32)
        bias_part = sb("bias_part", [3, 3, BIAS_MIX], BF16)
        bias_left = sb("bias_left", [3, 3, BIAS_MIX], F32)
        s_split = sem("weights_split")
        ln = Layernorm(sb, "tok_ln_")
        s_x = [sem(f"x_loaded{k}") for k in range(2)]
        s_xh, s_xs, s_xt, s_xk, s_vo, s_vk, s_tile, s_hi, s_lo = (sem(n) for n in (
            "x_high_made", "x_split_made", "x_turned", "xT_kept", "vo_made", "vo_kept", "qk_tile_made",
            "qk_high_kept", "qk_low_kept"))
        s_s, s_g, s_av, s_yT = (sem(n) for n in ("scores_made", "scores_gated", "products_made", "yT_kept"))
        s_y, s_h, s_hk, s_own, s_var, s_sd, s_nm, s_nh, s_n, s_nT, s_nk = (sem(n) for n in (
            "y_turned", "h_made", "h_stored", "tok_dve_step", "variance_made", "deviation_made", "normed_made",
            "normed_high_made", "normed_split_made", "tok_normed_turned", "tok_normed_kept"))

        QK_TILES = (("q", 0), ("k", 0), ("k", 1), ("q", 1))
        PE_TILE = {9: 0, 10: 1, 12: 2, 13: 3}
        DVE_TILE = {11: 0, 12: 1, 13: 2, 14: 3}
        past_first = lambda b: not (isinstance(b, int) and b == 0)

        def batches(engine, main, prep, post, finish=None):
            def pair(i, is_first=False, is_last=False):
                for k in range(2):
                    for t in range(NT):
                        if main:
                            main(i, k, t)
                        if not (is_first and k == 0):
                            post(2 * i + k - 1, 1 - k, t)
                        if not (is_last and k == 1):
                            prep(2 * i + k + 1, 1 - k, t)
                        if finish:
                            finish(i, k, t)
            pair(0, is_first=True)
            with engine.Fori(0, B // 2 - 2) as i:
                pair(i + 1)
            pair(B // 2 - 1, is_last=True)
            for t in range(NT):
                post(B - 1, 1, t)

        with nc.Block() as block:
            @block.sync
            def _(sp):
                def load(b, k):
                    sp.dma_start(x_rows[k][:], a["x"][b, 0].rearrange("(c p) d -> p c d", p=P)).then_inc(s_x[k], 16)

                def store_h(b):
                    sp.wait_ge(s_h, b + 1)
                    for half in range(2):
                        sp.dma_start(m.kept[b].rearrange("(half c p) d -> p half c d", half=2, p=P)[:, half],
                                     ln.h[:].rearrange("p (c half) d -> p half c d", half=2)[:, half]).then_inc(s_hk, 16)

                for k in range(2):
                    load(k, k)
                with sp.Fori(0, B // 2 - 1) as i:
                    for k in range(2):
                        sp.wait_ge(s_xs, 2 * i + k + 1)
                        load(2 * i + 2 + k, k)
                        store_h(2 * i + k)
                for b in range(B - 2, B):
                    store_h(b)
                sp.wait_ge(s_hk, 32 * B + 1)

            @block.gpsimd
            def _(pool):
                pool.wait_ge(m.s_raw, m.n_raw)
                split_weights(nc.gpsimd, Links(pool, s_split), m, bias_part, bias_left)

            @block.tensor
            def _(pe):
                bank, mm = m.bank, nc.tensor.matmul

                def scores(i, k, t):
                    half, s = divmod(t, NB)
                    n = 2 * NT * i + NT * k + t
                    if t in (0, 4, 8):
                        pe.wait_ge(s_lo, 8 * i + 4 * k + 2 + t // 4)
                    anew = k == 0 and t < 2
                    pe.wait_ge(s_g, n + (2 if anew else 1))
                    z = bank[(NT * k + t) % RING][:]
                    for q, stop in ((q_hi, False), (q_lo, True)):
                        last = mm(z, k_both[k][:, s * P:(s + 1) * P], q[k][:, half * HALF:(half + 1) * HALF],
                                  start=not stop, stop=stop)
                    last.then_inc(s_s, 1)

                def product(i, k, t):
                    half, s = divmod(t, NB)
                    if t == 0:
                        pe.wait_ge(s_vk, 2 * i + k + 1)
                        if past_first(i):
                            pe.wait_ge(s_yT, 2 * i + k - 1)
                    pe.wait_ge(s_g, 2 * NT * i + NT * k + t + 1 + RING)
                    mm(bank[3 + k][half * D:(half + 1) * D, :], vo[k][:, s, :], gated[:, (NT * k + t) % RING, :],
                       start=(s == 0), stop=(s == NB - 1)).then_inc(s_av, 1)

                def scores_ahead(i, k, t):
                    ahead = NT * k + t + 2
                    i, ahead = (i, ahead) if ahead < 2 * NT else (i + 1, ahead - 2 * NT)
                    if not (isinstance(i, int) and i == B // 2):
                        scores(i, ahead // NT, ahead % NT)

                def post(b, k, t):
                    if t == 1:
                        pe.wait_ge(s_yT, b + 1)
                        if past_first(b):
                            pe.wait_ge(s_nk, b)
                        for c in range(4):
                            last = nc.tensor.transpose(bank[7][:, c * P:(c + 1) * P], yT[:, c * P:(c + 1) * P],
                                                       m.ident[:])
                        last.then_inc(s_y, 1)
                    if t == 12:
                        pe.wait_ge(s_n, b + 1)
                        for q in range(NB):
                            at = TOKENS_OF[q] * P
                            last = nc.tensor.transpose(bank[7][:].bitcast(F16)[:, at:at + P], ln.split[:, q, :],
                                                       m.ident16[:])
                        last.then_inc(s_nT, 1)

                def prep(b, k, t):
                    if t == 2:
                        pe.wait_ge(s_xs, b + 1)
                        if past_first(b):
                            pe.wait_ge(s_lo, 4 * b - 1)
                        for c in range(NB):
                            last = nc.tensor.transpose(bank[5][:].bitcast(F16)[:, c * P:(c + 1) * P],
                                                       x_split[:, c, :], m.ident16[:])
                        last.then_inc(s_xt, 1)
                    if t == 5:
                        pe.wait_ge(s_xk, b + 1)
                        if past_first(b):
                            pe.wait_ge(s_lo, 4 * b)
                        for c in range(NB):
                            z = bank[6][:, c * D:(c + 1) * D]
                            mm(z, m.ones_s[:, 0:P], m.vo_bias, start=(c == 0), stop=False, skip_group_check=True)
                            for w in (m.wvo_hi, m.wvo_lo):
                                last = mm(z, xT[:, c * P:(c + 1) * P], w[:], start=False, stop=(w is m.wvo_lo),
                                          skip_group_check=True)
                        last.then_inc(s_vo, 1)
                    if t in PE_TILE:
                        n = PE_TILE[t]
                        which, half = QK_TILES[n]
                        if n < 2:
                            pe.wait_ge(s_vk if n else s_xk, b + 1)
                        else:
                            pe.wait_ge(s_lo, 4 * b + n - 1)
                        w_hi, w_lo, bias = (m.wq_hi, m.wq_lo, m.q_bias) if which == "q" else (m.wk_hi, m.wk_lo, m.k_bias)
                        z = bank[5 + n % 2][:]
                        x = xT[:, half * HALF:(half + 1) * HALF]
                        mm(z, bias, m.ones_s[:], start=True, stop=False)
                        mm(z, w_hi[:].rearrange("p two d -> p (two d)"), x, start=False, stop=False)
                        mm(z, w_lo[:].rearrange("p two d -> p (two d)"), x, start=False, stop=True).then_inc(s_tile, 1)

                for t in range(NT):
                    prep(0, 0, t)
                scores(0, 0, 0)
                scores(0, 0, 1)
                batches(pe, scores_ahead, prep, post, product)

            @block.scalar
            def _(act):
                S = nc.scalar

                def post(b, k, t):
                    if t == 0:
                        act.wait_ge(s_av, NT * (b + 1))
                        S.activation(yT[:], m.bank[3 + k][:], ACT.Identity, bias=m.bo_col[:, 0:1]).then_inc(s_yT, 1)
                    if t == 7:
                        act.wait_ge(s_var, b + 1)
                        S.activation(ln.dev[:], ln.var[:], ACT.Sqrt).then_inc(s_sd, 1)
                    if t == 9:
                        act.wait_ge(s_nm, b + 1)
                        S.activation(ln.split[:, :, 0:D], ln.square[:], ACT.Identity).then_inc(s_nh, 1)
                    if t == 13:
                        act.wait_ge(s_nT, b + 1)
                        S.copy(m.xs[:, COLS:COLS + T * B].rearrange("p (t b) -> p t b", b=B)[:, :, b],
                               m.bank[7][:].bitcast(F16)).then_inc(s_nk, 1)

                def prep(b, k, t):
                    if t == 0:
                        act.wait_ge(s_x[k], 8 * (b - k) + 16)
                        if past_first(b):
                            act.wait_ge(s_xt, b)
                        S.activation(x_split[:, :, 0:D], x_rows[k][:], ACT.Identity, scale=MIX_SCALE).then_inc(s_xh, 1)
                    if t == 2:
                        act.wait_ge(s_xt, b + 1)
                        S.copy(xT[:], m.bank[5][:].bitcast(F16)).then_inc(s_xk, 1)
                    if t == 5:
                        act.wait_ge(s_vo, b + 1)
                        S.activation(vo[k][:].rearrange("p c d -> p (c d)"), m.bank[6][:], ACT.Identity,
                                     scale=MIX_SCALE ** -4).then_inc(s_vk, 1)
                    if t in PE_TILE:
                        n = PE_TILE[t]
                        which, half = QK_TILES[n]
                        high = (q_hi if which == "q" else k_both)[k]
                        act.wait_ge(s_tile, 4 * b + n + 1)
                        S.activation(high[:, half * HALF:(half + 1) * HALF], m.bank[5 + n % 2][:], ACT.Identity,
                                     scale=1.0 / MIX_SCALE).then_inc(s_hi, 1)

                S.activation(hello[:, 0:1], m.ident[:, 0:1], ACT.Sqrt)
                for t in range(NT):
                    prep(0, 0, t)
                batches(act, None, prep, post)

            @block.vector
            def _(dve):
                V = nc.vector
                TT, TS, STT = V.tensor_tensor, V.tensor_scalar, V.scalar_tensor_tensor
                V.memset(hello[:, 1:2], 0.0).then_inc(s_g, RING)
                V.memset(hello[:, 2:3], 0.0).then_inc(s_hk, 1)

                def gate(i, k, t):
                    half, s = divmod(t, NB)
                    n = 2 * NT * i + NT * k + t
                    slot = (NT * k + t) % RING
                    dve.wait_ge(s_s, n + 1)
                    if k == 0 and t < 2 and past_first(i):
                        dve.wait_ge(s_av, n - 1)
                    TT(gated[:, slot, :], m.bank[slot][:], m.gT[:, s, half * HALF:(half + 1) * HALF], ALU.mult
                       ).then_inc(s_g, 1)

                latest = []

                def post(b, k, t):
                    if t == 2:
                        latest[:] = [Own(dve, s_own, LINKS * b)]
                        own = latest[0]
                        dve.wait_ge(s_y, b + 1)
                        own.made(TS(neg[:], m.bank[7][:].rearrange("p (c d) -> p c d", d=D), 0.0, m.a_col[:, 0:1],
                                    ALU.min, ALU.mult))
                    own = latest[0] if latest else None
                    if t == 3:
                        own.wait()
                        dve.wait_ge(s_hk, 32 * b + 1)
                        STT(ln.h[:], m.bank[7][:].rearrange("p (c d) -> p c d", d=D), 0.0, neg[:], ALU.max, ALU.add
                            ).then_inc(s_h, 1)
                    if t == 4:
                        dve.wait_ge(s_h, b + 1)
                        own.made(V.tensor_reduce(ln.total[:], ln.h[:], AX.X, ALU.add))
                        own.wait()
                        own.made(TS(ln.mean[:], ln.total[:], 1.0 / D, None, ALU.mult))
                    if t == 5:
                        own.wait()
                        own.made(TT(ln.centred[:], ln.h[:], over_tokens(ln.mean[:]), ALU.subtract))
                    if t == 6:
                        own.wait()
                        own.made(TT(ln.square[:], ln.centred[:], ln.centred[:], ALU.mult))
                    if t == 7:
                        own.wait()
                        own.made(V.tensor_reduce(ln.squares[:], ln.square[:], AX.X, ALU.add))
                        own.wait()
                        TS(ln.var[:], ln.squares[:], 1.0 / D, EPS, ALU.mult, ALU.add).then_inc(s_var, 1)
                    if t == 8:
                        dve.wait_ge(s_sd, b + 1)
                        own.made(V.reciprocal(ln.r0[:], ln.dev[:]))
                        own.wait()
                        own.made(TT(ln.t1[:], ln.r0[:], ln.r0[:], ALU.mult))
                        own.wait()
                        own.made(TT(ln.t2[:], ln.t1[:], ln.var[:], ALU.mult))
                        own.wait()
                        own.made(TS(ln.t3[:], ln.t2[:], -0.5 * X_SCALE, 1.5 * X_SCALE, ALU.mult, ALU.add))
                    if t == 9:
                        own.wait()
                        own.made(TT(ln.r[:], ln.r0[:], ln.t3[:], ALU.mult))
                        own.wait()
                        TT(ln.square[:], ln.centred[:], over_tokens(ln.r[:]), ALU.mult).then_inc(s_nm, 1)
                        assert own.n == LINKS, own.n
                    if t == 10:
                        dve.wait_ge(s_nh, b + 1)
                        TT(ln.split[:, :, D:2 * D], ln.square[:], ln.split[:, :, 0:D], ALU.subtract).then_inc(s_n, 1)

                def prep(b, k, t):
                    if t == 0:
                        dve.wait_ge(s_xh, b + 1)
                        STT(x_split[:, :, D:2 * D], x_rows[k][:], MIX_SCALE, x_split[:, :, 0:D], ALU.mult, ALU.subtract
                            ).then_inc(s_xs, 1)
                    if t in DVE_TILE:
                        n = DVE_TILE[t]
                        which, half = QK_TILES[n]
                        cols = slice(half * HALF, (half + 1) * HALF)
                        dve.wait_ge(s_hi, 4 * b + n + 1)
                        if which == "q":
                            low, high, z = q_lo[k][:, cols], q_hi[k][:, cols], m.bank[5 + n % 2][:]
                        else:
                            low = high = k_both[k][D:2 * D, cols]
                            z = m.bank[5 + n % 2][D:2 * D, :]
                        STT(low, z, 1.0 / MIX_SCALE, high, ALU.mult, ALU.subtract).then_inc(s_lo, 1)

                for t in range(NT):
                    prep(0, 0, t)
                batches(dve, gate, prep, post)


class Chain:

    def __init__(self, sb, sem, d, name):
        self.d = d
        self.tanh_fi = sb(f"tanh_fi_{name}", [P, 2, B], F32)
        self.planes = sb(f"planes_{name}", [P, 3, B, 2], F32)
        self.scanned = sb(f"scanned_{name}", [P, B, 2], F32)
        self.cell_one = sb(f"cell_one_{name}", [P, 2, B], F32)
        self.out_gate, self.tanh_cell, self.h = (
            sb(f"{part}_{name}", [P, B], F32) for part in ("out_gate", "tanh_cell", "h"))
        (self.s_z_fi, self.s_z_go, self.s_t_fi, self.s_t_go, self.s_terms, self.s_out_gate, self.s_scan,
         self.s_cell, self.s_tanh_cell, self.s_hi, self.s_h, self.s_lo) = (sem(f"{s}_{name}") for s in (
             "z_fi", "z_go", "t_fi", "t_go", "terms", "out_gate", "scan", "cell", "tanh_cell", "hi", "h", "lo"))

    def start(self, nc, own):
        own.link(nc.vector.memset(self.planes[:], 0.0))
        own.link(nc.vector.memset(self.scanned[:], 0.0))
        own.link(nc.vector.memset(self.cell_one[:, 1, :], 1.0))
        nc.vector.memset(self.cell_one[:, 0, :], 0.0).then_inc(self.s_cell, 1)



def pe_gates(nc, pe, m, c, n, h_hi, h_lo, fi, go):
    z = (fi[:, 0, :], fi[:, 1, :], go[:, 0, :], go[:, 1, :])
    pe.wait_ge(c.s_hi, n + 1)
    for w in (m.u_lo[c.d], m.u_hi[c.d]):
        for g in range(4):
            nc.tensor.matmul(z[g], w[:, g, :], h_hi, start=False, stop=False, skip_group_check=True)
    pe.wait_ge(c.s_lo, n + 1)
    for g in range(4):
        last = nc.tensor.matmul(z[g], m.u_hi[c.d][:, g, :], h_lo, start=False, stop=True, skip_group_check=True)
        if g == I_:
            last.then_inc(c.s_z_fi, 1)
    last.then_inc(c.s_z_go, 1)


def act_gates(nc, act, c, n, fi, go):
    act.wait_ge(c.s_z_fi, n + 1)
    nc.scalar.activation(c.tanh_fi[:], fi, ACT.Tanh, scale=1.0 / Z_SCALE).then_inc(c.s_t_fi, 1)
    act.wait_ge(c.s_z_go, n + 1)
    nc.scalar.activation(c.planes[:, 0:3:2, :, 0], go, ACT.Tanh, scale=1.0 / Z_SCALE).then_inc(c.s_t_go, 1)


def act_cell(nc, act, c, n):
    act.wait_ge(c.s_scan, n + 1)
    nc.scalar.activation(c.tanh_cell[:], c.scanned[:, :, 1], ACT.Tanh, scale=0.5).then_inc(c.s_tanh_cell, 1)


def dve_terms(nc, dve, c, n):
    dve.wait_ge(c.s_t_fi, n + 1)
    dve.wait_ge(c.s_cell, n + 1)
    nc.vector.scalar_tensor_tensor(c.planes[:, 0:2, :, 1], c.tanh_fi[:], 1.0, c.cell_one[:], ALU.add, ALU.mult
                                   ).then_inc(c.s_terms, 1)


def dve_scan(nc, dve, c, n):
    dve.wait_ge(c.s_terms, n + 1)
    dve.wait_ge(c.s_t_go, n + 1)
    pairs = lambda z: z.rearrange("p b two -> p (b two)")
    nc.vector.tensor_tensor_scan(pairs(c.scanned[:]), pairs(c.planes[:, 1]), pairs(c.planes[:, 0]), 0.0,
                                 ALU.mult, ALU.add).then_inc(c.s_scan, 1)


def dve_rest(nc, dve, c, scans):
    nc.vector.tensor_scalar(c.out_gate[:], c.planes[:, 2, :, 0], 1.0, 0.5 * X_SCALE, ALU.add, ALU.mult
                            ).then_inc(c.s_out_gate, 1)
    dve.wait_ge(c.s_scan, scans)
    nc.vector.tensor_scalar(c.cell_one[:, 0, :], c.scanned[:, :, 1], 0.5, None, ALU.mult).then_inc(c.s_cell, 1)


def dve_hidden(nc, dve, c, n, h_hi):
    tt = nc.vector.tensor_tensor
    tt(h_hi, c.out_gate[:], c.tanh_cell[:], ALU.mult).then_inc(c.s_hi, 1)
    tt(c.h[:], c.out_gate[:], c.tanh_cell[:], ALU.mult).then_inc(c.s_h, 1)


def dve_hidden_low(nc, dve, c, n, h_hi, h_lo):
    dve.wait_ge(c.s_h, n + 1)
    nc.vector.tensor_tensor(h_lo, c.h[:], h_hi, ALU.subtract).then_inc(c.s_lo, 1)


def encoder(nc, m):
    ctx, sb, sem = tools(nc)
    with ctx:
        ch = [Chain(sb, sem, d, name) for d, name in enumerate(("fwd", "bwd"))]
        s_set = sem("encoder_state_set")
        hello = sb("encoder_hello", [P, 1], F32)
        h = list(zip(m.enc_hi, m.enc_lo))

        banks = [[[m.bank[4 * d + 2 * p + j][:].rearrange("p (g t b) -> p g t b", g=2, t=CH) for j in range(2)]
                  for p in range(2)] for d in range(2)]

        def at(d, step):
            p, s = divmod(step, CH)
            s = CH - 1 - s if d else s
            return [z[:, :, s, :] for z in banks[d][p]]

        with nc.Block() as block:
            @block.tensor
            def _(pe):
                def fill(d, p, unit, col):
                    g, half = divmod(unit, 2)
                    z = banks[d][p][g // 2][:, g % 2, half * CH // 2:(half + 1) * CH // 2, :]
                    nc.tensor.matmul(z, m.w_hi[d][:, g, :], m.xs[:, bass.ds(col, HALFCH)],
                                     start=(unit % 4 == 0), stop=False, skip_group_check=True)
                    nc.tensor.matmul(z, m.w_lo[d][:, g, :], m.xs[:, bass.ds(col, HALFCH)],
                                     start=False, stop=False, skip_group_check=True)
                    nc.tensor.matmul(z, m.lstm_bias[d][:, GATE_FROM[g], :], m.ones3[:],
                                     start=False, stop=False, skip_group_check=True)

                for d in range(2):
                    for unit in range(8):
                        fill(d, 0, unit, COLS + (NCH - 1) * COLS * d + (unit % 2) * HALFCH)
                with pe.Fori(0, NCH // 2) as i:
                    for step in range(2 * CH):
                        p, s = divmod(step, CH)
                        for d in range(2):
                            fi, go = at(d, step)
                            pe_gates(nc, pe, m, ch[d], 2 * CH * i + step, h[d][0][:], h[d][1][:], fi, go)
                            if s % 2 == d:
                                unit = s // 2
                                col = (unit % 2) * HALFCH + (COLS * (NCH - 1 - p) - 2 * COLS * i if d else
                                                            COLS * (2 + p) + 2 * COLS * i)
                                fill(d, 1 - p, unit, col)

            @block.scalar
            def _(act):
                nc.scalar.activation(hello[:], m.ident[:, 0:1], ACT.Gelu)
                with act.Fori(0, NCH // 2) as i:
                    for step in range(2 * CH):
                        n = 2 * CH * i + step
                        act_cell(nc, act, ch[1], n)
                        act_gates(nc, act, ch[0], n, *at(0, step))
                        act_cell(nc, act, ch[0], n)
                        act_gates(nc, act, ch[1], n, *at(1, step))
                act_cell(nc, act, ch[1], T)

            @block.vector
            def _(dve):
                own = Links(dve, s_set)
                for d in range(2):
                    ch[d].start(nc, own)
                nc.vector.memset(ch[1].out_gate[:], 0.0).then_inc(ch[1].s_out_gate, 1)
                nc.vector.memset(h[0][0][:], 0.0).then_inc(ch[0].s_hi, 1)
                nc.vector.memset(h[0][1][:], 0.0).then_inc(ch[0].s_lo, 1)
                nc.vector.memset(ch[1].h[:], 0.0).then_inc(ch[1].s_scan, 1)

                def hidden(late, n):
                    dve.wait_ge(ch[late].s_tanh_cell, n + 1)
                    dve.wait_ge(ch[late].s_out_gate, n + 1)
                    dve_hidden(nc, dve, ch[late], n, h[late][0][:])

                with dve.Fori(0, NCH // 2) as i:
                    for step in range(2 * CH):
                        n = 2 * CH * i + step
                        for d in range(2):
                            late = 1 - d
                            hidden(late, n)
                            dve_terms(nc, dve, ch[d], n)
                            dve_hidden_low(nc, dve, ch[late], n, h[late][0][:], h[late][1][:])
                            dve_scan(nc, dve, ch[d], n)
                            dve_rest(nc, dve, ch[d], n + 1 + d)
                hidden(1, T)
                dve_hidden_low(nc, dve, ch[1], T, h[1][0][:], h[1][1][:])


BODY = 32
QS = BODY * B // P
LANES = P // B
RSQRT_SEED = 0x5f3759df


def decoder_and_experts(nc, m):
    ctx, sb, sem = tools(nc)
    with ctx:
        c = Chain(sb, sem, 2, "dec")
        ring_hi = sb("ring_hi", [P, QS, B, LANES], F16)
        ring_lo = sb("ring_lo", [P, QS, B, LANES], F16)
        h_at = lambda ring, step: ring[:, step % QS, :, step % BODY // QS]
        given = sb("given", [P, 4 * B], F32)
        left = sb("given_left", [P, 2, 4 * B], F32)
        parts = sb("given_parts", [P, 3, 4, B], BF16)
        s_given, s_parts, s_set = (sem(n) for n in ("given_made", "given_split", "decoder_set"))
        banks = [[m.bank[2 * p + j][:].rearrange("p (g t b) -> p g t b", g=2, t=CH) for j in range(2)]
                 for p in range(2)]

        wide = lambda name: sb(name, [P, QS, D], F32)
        one = lambda name: sb(name, [P, QS], F32)
        each = lambda name: sb("route_" + name, [P, QS, E], F32)
        res, h, h_kept, centred, square, normed, sums = (wide(n) for n in (
            "res", "ff_h", "ff_h_kept", "centred", "square", "normed", "sums"))
        split = sb("split", [P, QS, 2 * D], F16)
        total, mean, squares, var, half_bits, seed = (one(n) for n in (
            "total", "mean", "squares", "var", "half_bits", "rsqrt0"))
        newton = [[one(f"newton{k}_{part}") for part in ("square", "term", "rsqrt")] for k in range(3)]
        rank = sb("rank", [P, E], F32)
        rank_int = sb("rank_int", [P, E], mybir.dt.int32)
        score, equal0, ranked0, first, others, equal1, ranked1, second, chosen = (each(n) for n in (
            "score", "equal0", "ranked0", "first", "others", "equal1", "ranked1", "second", "chosen"))
        best = [one(f"best{k}") for k in range(4)]
        mask = sb("mask", [P, QS, 2 * E], BF16)
        xn = sb("xn", [P, HALF], F16)
        maskT = sb("maskT", [2 * E, HALF], BF16)
        hid = sb("hid", [HE, 2, HALF], F32)
        yT = sb("ff_yT", [D, HALF], F32)
        s_own = sem("ff_dve_step")
        (s_res, s_proj, s_normed, s_high, s_h, s_hk, s_split, s_nT, s_xn, s_score, s_mask, s_mT, s_mk, s_pre, s_hid,
         s_y, s_yT, s_yt, s_sum, s_out, s_rank) = (sem(n) for n in (
             "res_loaded", "projected", "normed_made", "normed_high_made", "ff_h_made", "ff_h_kept", "normed_split", "normed_turned",
             "xn_kept", "gate_scores", "mask_made", "mask_turned", "maskT_kept", "pre_made", "hid_made",
             "ff_y_made", "yT_kept", "y_turned", "sum_made", "sum_stored", "rank_made"))

        def tile_rows(tensor, j):
            return tensor.rearrange("b (j u c) d -> j b u (c d)", u=LANES, c=QS)[bass.ds(j, 1)]

        def past_first(j):
            return not (isinstance(j, int) and j == 0)

        flat = lambda z: z[:].rearrange("p c d -> p (c d)")
        NJ = T // BODY
        DVE_OWN = 31
        small = m.bank[4]
        y_bank = m.bank[7]
        pre_bank = [m.bank[5], m.bank[6]]
        over_d = lambda col: col[:].unsqueeze(2).broadcast_to([P, QS, D])
        over_e = lambda col: col[:].unsqueeze(2).broadcast_to([P, QS, E])

        def at(step):
            p, s = divmod(step, CH)
            return [z[:, :, s, :] for z in banks[p]]

        def bodies(engine, body):
            body(0, [])
            body(1, [(0, 0)])
            with engine.Fori(0, NJ - 2) as i:
                body(i + 2, [(i, BODY), (i + 1, 0)])

        def after(part):
            for s in range(2 * BODY):
                if s < BODY:
                    part(NJ - 2, s + BODY)
                part(NJ - 1, s)

        with nc.Block() as block:
            @block.sync
            def _(sp):
                def load(j):
                    sp.dma_start(flat(res), tile_rows(m.kept, j)).then_inc(s_res, 16)

                def store(j):
                    sp.wait_ge(s_sum, j + 1)
                    sp.dma_start(tile_rows(m.out, j), flat(sums)).then_inc(s_out, 16)

                load(0)
                sp.wait_ge(s_h, 1)
                load(1)
                with sp.Fori(0, NJ - 2) as i:
                    sp.wait_ge(s_h, i + 2)
                    load(i + 2)
                    store(i)
                store(NJ - 2)
                store(NJ - 1)
                sp.wait_ge(s_out, 16 * NJ + 1)

            @block.gpsimd
            def _(pool):
                G = nc.gpsimd
                G.iota(rank_int[:], pattern=[[-1, E]], base=E, channel_multiplier=0).then_inc(s_rank, 1)
                pool.wait_ge(s_rank, 1)
                G.tensor_copy(rank[:], rank_int[:]).then_inc(s_rank, 1)

            @block.tensor
            def _(pe):
                mm = nc.tensor.matmul

                def fill(p, unit):
                    g, half = divmod(unit, 2)
                    z = banks[p][g // 2][:, g % 2, half * CH // 2:(half + 1) * CH // 2, :]
                    for k in range(3):
                        mm(z, m.identb[:], parts[:, k, g, :].unsqueeze(1).broadcast_to([P, CH // 2, B]),
                           start=(unit % 4 == 0 and k == 0), stop=False, skip_group_check=True)

                def pre_x(j, e):
                    if e < 2:
                        if e == 0 and past_first(j):
                            pe.wait_ge(s_sum, j)
                    else:
                        pe.wait_ge(s_hid, E * j + e - 1)
                    mm(pre_bank[e % 2][:], m.w1_hi[:, e, :], xn[:], start=True, stop=False)
                    mm(pre_bank[e % 2][:], m.w1_lo[:, e, :], xn[:], start=False, stop=False)

                def pre_mask(j, e):
                    mm(pre_bank[e % 2][:], m.pick[:, e, :], maskT[:], start=False, stop=True).then_inc(s_pre, 1)

                def pe_part(j, s):
                    if s in (0, 1):
                        if s == 0:
                            pe.wait_ge(c.s_lo, BODY * (j + 1) + 1)
                        for blk in (2 * s, 2 * s + 1):
                            z = small[:, blk * D:(blk + 1) * D]
                            mm(z, m.ones3[:], m.wo_bias, start=(blk == 0), stop=False, skip_group_check=True)
                            for ring, wo in ((ring_hi, m.wo_hi), (ring_hi, m.wo_lo), (ring_lo, m.wo_hi)):
                                last = mm(z, ring[:, blk].rearrange("p b u -> p (b u)"), wo[:], start=False, stop=True, skip_group_check=True)
                        last.then_inc(s_proj, 1)
                    if s == 11:
                        pe.wait_ge(s_split, j + 1)
                        for blk in range(QS):
                            last = nc.tensor.transpose(
                                small[:, HALF // 2:].bitcast(F16)[:, blk * P:(blk + 1) * P], split[:, blk, :],
                                m.ident16[:])
                        last.then_inc(s_nT, 1)
                    if s == 12:
                        pe.wait_ge(s_xn, j + 1)
                        for blk in range(QS):
                            x, z = xn[:, blk * P:(blk + 1) * P], small[:, blk * E:(blk + 1) * E]
                            mm(z, m.ones3[:], m.gate_bias, start=(blk == 0), stop=False, skip_group_check=True)
                            mm(z, x, m.wg_hi[:], start=False, stop=False, skip_group_check=True)
                            last = mm(z, x, m.wg_lo[:], start=False, stop=True, skip_group_check=True)
                        last.then_inc(s_score, 1)
                    if s in (14, 15):
                        pre_x(j, s - 14)
                    if s == 17:
                        pe.wait_ge(s_mask, j + 1)
                        for blk in range(QS):
                            last = nc.tensor.transpose(
                                small[:, HALF // 2:].bitcast(BF16)[0:2 * E, blk * P:(blk + 1) * P], mask[:, blk, :],
                                m.identb[:])
                        last.then_inc(s_mT, 1)
                    if s == 18:
                        pe.wait_ge(s_mk, j + 1)
                        pre_mask(j, 0)
                    if s == 19:
                        pre_mask(j, 1)
                    if s in (33, 35):
                        for part in ((0, 1) if s == 33 else (2,)):
                            last = mm(y_bank[0:D, :], m.b2[:, part, :], maskT[:], start=False, stop=(part == 2),
                                      skip_group_check=True)
                        if s == 35:
                            last.then_inc(s_y, 1)
                    if s in (19, 20):
                        pe.wait_ge(s_hid, E * j + 1)
                        cols = slice((s - 19) * HALF // 2, (s - 18) * HALF // 2)
                        mm(y_bank[0:D, cols], m.w2[:, 0, :], hid[:, 0, cols], start=(s == 19), stop=False,
                           skip_group_check=True)
                    if 21 <= s < 20 + 2 * E:
                        e, odd = divmod(s - 20, 2)
                        if not odd:
                            pe.wait_ge(s_hid, E * j + e + 1)
                            mm(y_bank[0:D, :], m.w2[:, e, :], hid[:, e % 2, :], start=False, stop=False,
                               skip_group_check=True)
                        elif e + 2 < E:
                            pre_x(j, e + 2)
                            pre_mask(j, e + 2)
                    if s in (37, 38):
                        if s == 37:
                            pe.wait_ge(s_yT, j + 1)
                        for blk in range(2 * (s - 37), 2 * (s - 37) + 2):
                            last = mm(pre_bank[0][:, blk * D:(blk + 1) * D], yT[:, blk * P:(blk + 1) * P],
                                      m.ident[0:D, 0:D], start=(blk == 0), stop=True, skip_group_check=True)
                        if s == 38:
                            last.then_inc(s_yt, 1)

                z = m.bank[4][:, 0:4 * B]
                for g in range(4):
                    zg = z[:, g * B:(g + 1) * B]
                    first_of_bank = g == 0
                    for d in range(2):
                        for w, v in ((m.wd_hi, m.enc_hi), (m.wd_lo, m.enc_hi), (m.wd_hi, m.enc_lo)):
                            mm(zg, w[d][:, g, :], v[d][:], start=first_of_bank, stop=False, skip_group_check=True)
                            first_of_bank = False
                    last = mm(zg, m.lstm_bias[2][:, GATE_FROM[g], :], m.ones3[:, 0:B], start=False, stop=True,
                              skip_group_check=True)
                last.then_inc(s_given, 1)
                pe.wait_ge(s_parts, 1)
                for unit in range(8):
                    fill(0, unit)

                def body(i, tiles):
                    for step in range(BODY):
                        p, s = divmod(step, CH)
                        before = (step - 1) % BODY
                        pe_gates(nc, pe, m, c, BODY * i + step, h_at(ring_hi, before), h_at(ring_lo, before), *at(step))
                        if s % 2:
                            fill(1 - p, s // 2)
                        for j, start in tiles:
                            pe_part(j, start + step)

                bodies(pe, body)
                after(pe_part)

            @block.scalar
            def _(act):
                S = nc.scalar

                def act_part(j, s):
                    if s == 10:
                        act.wait_ge(s_normed, j + 1)
                        S.activation(split[:, :, 0:D], normed[:], ACT.Identity, scale=X_SCALE).then_inc(s_high, 1)
                    if s == 11:
                        act.wait_ge(s_nT, j + 1)
                        S.copy(xn[:], small[:, HALF // 2:].bitcast(F16)).then_inc(s_xn, 1)
                    if s == 13:
                        act.wait_ge(s_h, j + 1)
                        if past_first(j):
                            act.wait_ge(s_sum, j)
                        S.copy(h_kept[:], h[:]).then_inc(s_hk, 1)
                    if s == 17:
                        act.wait_ge(s_mT, j + 1)
                        S.copy(maskT[:], small[:, HALF // 2:].bitcast(BF16)[0:2 * E, :]).then_inc(s_mk, 1)
                    if s in range(18, 18 + 2 * E, 2):
                        e = (s - 18) // 2
                        act.wait_ge(s_pre, E * j + e + 1)
                        S.activation(hid[:, e % 2, :], pre_bank[e % 2][:], ACT.Gelu, scale=1.0 / Z_SCALE,
                                     bias=m.b1[:, e:e + 1]).then_inc(s_hid, 1)
                    if s == 36:
                        act.wait_ge(s_y, j + 1)
                        S.copy(yT[:], y_bank[0:D, :]).then_inc(s_yT, 1)

                def body(i, tiles):
                    for step in range(BODY):
                        n = BODY * i + step
                        act_gates(nc, act, c, n, *at(step))
                        act_cell(nc, act, c, n)
                        for j, start in tiles:
                            act_part(j, start + step)

                bodies(act, body)
                after(act_part)

            @block.vector
            def _(dve):
                V = nc.vector
                own = Links(dve, s_set)
                c.start(nc, own)
                V.memset(sums[:], 0.0).then_inc(s_out, 1)
                V.memset(h_at(ring_hi, BODY - 1), 0.0).then_inc(c.s_hi, 1)
                V.memset(h_at(ring_lo, BODY - 1), 0.0).then_inc(c.s_lo, 1)
                dve.wait_ge(s_given, 1)
                own.link(V.tensor_copy(given[:], m.bank[4][:, 0:4 * B]))
                third = parts[:].rearrange("p k g b -> p k (g b)")
                own.link(V.tensor_copy(third[:, 0], given[:]))
                own.link(V.tensor_tensor(left[:, 0], given[:], third[:, 0], ALU.subtract))
                own.link(V.tensor_copy(third[:, 1], left[:, 0]))
                own.link(V.tensor_tensor(left[:, 1], left[:, 0], third[:, 1], ALU.subtract))
                V.tensor_copy(third[:, 2], left[:, 1]).then_inc(s_parts, 1)
                dve.wait_ge(s_rank, 2)

                TT, TS, STT, RED = V.tensor_tensor, V.tensor_scalar, V.scalar_tensor_tensor, V.tensor_reduce
                ranks = rank[:].unsqueeze(1).broadcast_to([P, QS, E])
                INT = mybir.dt.int32

                def in_gates(j, s, own):
                    do = own.made
                    if s == 1:
                        dve.wait_ge(s_proj, 2 * j + 2)
                        dve.wait_ge(s_res, 16 * j + 16)
                        if past_first(j):
                            dve.wait_ge(s_hk, j)
                        STT(flat(h), small[:, 0:QS * D], 1.0 / Z_SCALE, flat(res), ALU.mult, ALU.add).then_inc(s_h, 1)
                    if s == 2:
                        dve.wait_ge(s_h, j + 1)
                        do(RED(total[:], h[:], AX.X, ALU.add))
                        own.wait()
                        do(TS(mean[:], total[:], 1.0 / D, None, ALU.mult))
                    if s == 3:
                        own.wait()
                        do(TT(centred[:], h[:], over_d(mean), ALU.subtract))
                    if s == 4:
                        own.wait()
                        do(TT(square[:], centred[:], centred[:], ALU.mult))
                    if s == 5:
                        own.wait()
                        do(RED(squares[:], square[:], AX.X, ALU.add))
                        own.wait()
                        do(TS(var[:], squares[:], 1.0 / D, EPS, ALU.mult, ALU.add))
                    if s == 6:
                        own.wait()
                        do(TS(seed[:].bitcast(INT), half_bits[:].bitcast(INT), -1.0, float(RSQRT_SEED), ALU.mult, ALU.add))
                        newton_square(own, 0)
                        newton_term(own, 0)
                    if s == 7:
                        newton_square(own, 1)
                        newton_term(own, 1)
                        newton_last(own, 1)
                    if s == 8:
                        newton_term(own, 2)
                        newton_last(own, 2)
                    if s == 9:
                        own.wait()
                        TT(normed[:], centred[:], over_d(newton[2][2]), ALU.mult).then_inc(s_normed, 1)
                    if s == 10:
                        dve.wait_ge(s_high, j + 1)
                        STT(split[:, :, D:2 * D], normed[:], X_SCALE, split[:, :, 0:D], ALU.mult, ALU.subtract
                            ).then_inc(s_split, 1)
                    if s == 12:
                        dve.wait_ge(s_score, j + 1)
                        do(V.tensor_copy(score[:], small[:, 0:QS * E].rearrange("p (q e) -> p q e", e=E)))
                        own.wait()
                        do(RED(best[0][:], score[:], AX.X, ALU.max))
                        own.wait()
                        do(TT(equal0[:], score[:], over_e(best[0]), ALU.is_equal))
                    if s == 13:
                        own.wait()
                        do(RED(best[1][:], ranked0[:], AX.X, ALU.max))
                        own.wait()
                        do(TT(first[:], ranked0[:], over_e(best[1]), ALU.is_equal))
                        own.wait()
                        do(STT(others[:], first[:], -3e38, score[:], ALU.mult, ALU.add))
                    if s == 14:
                        own.wait()
                        do(TT(equal1[:], others[:], over_e(best[2]), ALU.is_equal))
                        own.wait()
                        do(TT(ranked1[:], equal1[:], ranks, ALU.mult))
                        own.wait()
                        do(RED(best[3][:], ranked1[:], AX.X, ALU.max))
                    if s == 15:
                        own.wait()
                        do(TT(chosen[:], first[:], second[:], ALU.add))
                        own.wait()
                        do(TS(mask[:, :, 0:E], chosen[:], -1.0, None, ALU.add))
                        V.tensor_copy(mask[:, :, E:2 * E], chosen[:]).then_inc(s_mask, 1)
                        assert own.n == DVE_OWN, own.n
                    if s == 43:
                        dve.wait_ge(s_yt, j + 1)
                        dve.wait_ge(s_hk, j + 1)
                        dve.wait_ge(s_out, 16 * j + 1)
                        TT(flat(sums), pre_bank[0][:, 0:QS * D], flat(h_kept), ALU.add).then_inc(s_sum, 1)

                def newton_square(own, k):
                    own.wait()
                    r = newton[k - 1][2] if k else seed
                    own.made(TT(newton[k][0][:], r[:], r[:], ALU.mult))

                def newton_term(own, k):
                    own.wait()
                    own.made(STT(newton[k][1][:], newton[k][0][:], -0.5, var[:], ALU.mult, ALU.mult))

                def newton_last(own, k):
                    own.wait()
                    r = newton[k - 1][2] if k else seed
                    own.made(STT(newton[k][2][:], newton[k][1][:], 1.5, r[:], ALU.add, ALU.mult))

                def in_tanh(j, s, own):
                    do = own.made
                    if s == 6:
                        own.wait()
                        do(TS(half_bits[:].bitcast(INT), var[:].bitcast(INT), 1, None, ALU.logical_shift_right))
                    if s == 7:
                        newton_last(own, 0)
                    if s == 8:
                        newton_square(own, 2)
                    if s == 13:
                        own.wait()
                        do(TT(ranked0[:], equal0[:], ranks, ALU.mult))
                    if s == 14:
                        own.wait()
                        do(RED(best[2][:], others[:], AX.X, ALU.max))
                    if s == 15:
                        own.wait()
                        do(TT(second[:], ranked1[:], over_e(best[3]), ALU.is_equal))

                def part(window, tiles, step):
                    for j, start, own in tiles:
                        window(j, start + step, own)

                def body(i, tiles):
                    tiles = [(j, start, Own(dve, s_own, DVE_OWN * j)) for j, start in tiles]
                    for step in range(BODY):
                        n = BODY * i + step
                        dve_terms(nc, dve, c, n)
                        dve_scan(nc, dve, c, n)
                        dve_rest(nc, dve, c, n + 1)
                        part(in_tanh, tiles, step)
                        if step < QS and step % 2 == 0 and tiles:
                            dve.wait_ge(s_proj, 2 * tiles[-1][0] + step // 2 + 1)
                        dve.wait_ge(c.s_tanh_cell, n + 1)
                        dve.wait_ge(c.s_out_gate, n + 1)
                        dve_hidden(nc, dve, c, n, h_at(ring_hi, step))
                        dve_hidden_low(nc, dve, c, n, h_at(ring_hi, step), h_at(ring_lo, step))
                        part(in_gates, tiles, step)

                bodies(dve, body)
                owns = {}

                def last_part(j, s):
                    if s in (0, BODY):
                        owns[j] = Own(dve, s_own, DVE_OWN * j)
                    in_tanh(j, s, owns[j])
                    in_gates(j, s, owns[j])
                after(last_part)


def kernel(**inputs):
    import numpy as _np
    import concourse.bacc as _bacc
    from concourse import mybir as _mybir
    from concourse.bass_utils import run_bass_kernel_spmd as _run

    nc = _bacc.Bacc("TRN2", target_bir_lowering=False, num_devices=1)
    arrays, args = {}, {}
    for name in sorted(inputs):
        array = _np.ascontiguousarray(inputs[name])
        arrays[f"in_{name}_dram"] = array
        args[name] = nc.dram_tensor(f"in_{name}_dram", array.shape, _mybir.dt.from_np(array.dtype),
                                    kind="ExternalInput").ap()
    out = nc.dram_tensor("out_dram", (B, T, D), _mybir.dt.float32, kind="ExternalOutput").ap()
    build(nc, args, out)
    r = _run(nc, [arrays], core_ids=[0])
    return r.results[0]["out_dram"]
```
